# Optimizing a Trainium2 kernel written in Bass

```python
import numpy as np
import jax
import jax.numpy as jnp

def _softmax(x, axis=-1):
    return jax.nn.softmax(x, axis=axis)

def _gelu(x):
    return jax.nn.gelu(x, approximate=True)

def _silu(x):
    return jax.nn.silu(x)

def _sigmoid(x):
    return jax.nn.sigmoid(x)

def _layernorm(x, axis=-1, eps=1e-05):
    m = jnp.mean(x, axis=axis, keepdims=True)
    v = jnp.var(x, axis=axis, keepdims=True)
    return (x - m) / jnp.sqrt(v + eps)

def _scatter_add(tgt, idx, src, axis=0):
    return tgt.at[idx].add(src)

def _segment_sum(src, seg, n):
    return jax.ops.segment_sum(src, seg, n)
kernel_name = 'mk_seq_postln_d1_jaxref_r8_24fc2b'

def setup_inputs(seed: int=0):
    np.random.seed(seed)
    _w = jnp.asarray

    def _L0_attn_setup():
        import jax, jax.numpy as jnp
        import numpy as np
        D_MODEL = 128
        D_INNER = 256
        D_STATE = 16
        D_CONV = 4
        DT_RANK = 64
        BATCH = 2
        SEQ = 128

        def _silu(v):
            return v * jax.nn.sigmoid(v)
        key = jax.random.key(seed)
        ks = jax.random.split(key, 8)
        s = 0.02
        return {'x': jax.random.normal(ks[0], (BATCH, SEQ, D_MODEL), jnp.float32), 'norm_w': jnp.ones((D_MODEL,), jnp.float32), 'in_proj_w': jax.random.normal(ks[1], (2 * D_INNER, D_MODEL), jnp.float32) * s, 'conv_w': jax.random.normal(ks[2], (D_INNER, 1, D_CONV), jnp.float32) * s, 'conv_b': jnp.zeros((D_INNER,), jnp.float32), 'x_proj_w': jax.random.normal(ks[3], (DT_RANK + 2 * D_STATE, D_INNER), jnp.float32) * s, 'dt_proj_w': jax.random.normal(ks[4], (D_INNER, DT_RANK), jnp.float32) * s, 'dt_proj_b': jnp.zeros((D_INNER,), jnp.float32), 'A_log': jnp.log(jnp.broadcast_to(jnp.arange(1, D_STATE + 1, dtype=jnp.float32), (D_INNER, D_STATE))), 'D': jnp.ones((D_INNER,), jnp.float32), 'out_proj_w': jax.random.normal(ks[5], (D_MODEL, D_INNER), jnp.float32) * s}
    _L0_attn_in = _L0_attn_setup()

    def _L0_ffn_setup():
        import jax, jax.numpy as jnp
        import numpy as np
        DIM = 128
        HIDDEN = 384
        SCALE = 1.0 / 127.0

        def _dequant(w_int, dtype):
            return w_int.astype(dtype) * jnp.asarray(SCALE, dtype)
        key = jax.random.key(seed)
        k_x, k_g, k_u, k_d = jax.random.split(key, 4)
        x = jax.random.normal(k_x, (4, 256, DIM), dtype=jnp.float32)
        w_gate = jax.random.randint(k_g, (HIDDEN, DIM), -127, 128, dtype=jnp.int32)
        w_up = jax.random.randint(k_u, (HIDDEN, DIM), -127, 128, dtype=jnp.int32)
        w_down = jax.random.randint(k_d, (DIM, HIDDEN), -127, 128, dtype=jnp.int32)
        return {'x': x, 'w_gate': w_gate, 'w_up': w_up, 'w_down': w_down}
    _L0_ffn_in = _L0_ffn_setup()
    _d = {'L0_attn_x': _L0_attn_in['x'], 'L0_attn_norm_w': _L0_attn_in['norm_w'], 'L0_attn_in_proj_w': _L0_attn_in['in_proj_w'], 'L0_attn_conv_w': _L0_attn_in['conv_w'], 'L0_attn_conv_b': _L0_attn_in['conv_b'], 'L0_attn_x_proj_w': _L0_attn_in['x_proj_w'], 'L0_attn_dt_proj_w': _L0_attn_in['dt_proj_w'], 'L0_attn_dt_proj_b': _L0_attn_in['dt_proj_b'], 'L0_attn_A_log': _L0_attn_in['A_log'], 'L0_attn_D': _L0_attn_in['D'], 'L0_attn_out_proj_w': _L0_attn_in['out_proj_w'], 'L0_ffn_w_gate': _L0_ffn_in['w_gate'], 'L0_ffn_w_up': _L0_ffn_in['w_up'], 'L0_ffn_w_down': _L0_ffn_in['w_down']}
    _x0 = _d['L0_attn_x']
    _d['L0_attn_x'] = jax.random.normal(jax.random.fold_in(jax.random.key(seed), 1), (8, 512, 128), dtype=_x0.dtype)
    del _x0
    return _d

def reference(L0_attn_x, L0_attn_norm_w, L0_attn_in_proj_w, L0_attn_conv_w, L0_attn_conv_b, L0_attn_x_proj_w, L0_attn_dt_proj_w, L0_attn_dt_proj_b, L0_attn_A_log, L0_attn_D, L0_attn_out_proj_w, L0_ffn_w_gate, L0_ffn_w_up, L0_ffn_w_down):

    def _L0_attn_ref(x, norm_w, in_proj_w, conv_w, conv_b, x_proj_w, dt_proj_w, dt_proj_b, A_log, D, out_proj_w):
        import jax, jax.numpy as jnp
        import numpy as np
        D_MODEL = 128
        D_INNER = 256
        D_STATE = 16
        D_CONV = 4
        DT_RANK = 64
        BATCH = 2
        SEQ = 128

        def _silu(v):
            return v * jax.nn.sigmoid(v)
        b, l, d = x.shape
        x_copy = x
        h = x * jax.lax.rsqrt(jnp.mean(x * x, axis=-1, keepdims=True) + 1e-05) * norm_w
        x_and_res = h @ in_proj_w.T
        xs, res = jnp.split(x_and_res, 2, axis=-1)
        xc = jnp.transpose(xs, (0, 2, 1))
        xc = jax.lax.conv_general_dilated(xc, conv_w, window_strides=(1,), padding=[(D_CONV - 1, 0)], feature_group_count=D_INNER, dimension_numbers=('NCH', 'OIH', 'NCH'))
        xc = xc + conv_b[None, :, None]
        u = _silu(jnp.transpose(xc, (0, 2, 1)))
        A = -jnp.exp(A_log)
        x_dbl = u @ x_proj_w.T
        delta, Bm, Cm = jnp.split(x_dbl, [DT_RANK, DT_RANK + D_STATE], axis=-1)
        delta = jax.nn.softplus(delta @ dt_proj_w.T + dt_proj_b)
        deltaA = jnp.exp(jnp.einsum('bld,dn->bldn', delta, A))
        deltaB_u = (delta * u)[..., None] * Bm[:, :, None, :]

        def step(state, inp):
            dA, dBu, c = inp
            state = dA * state + dBu
            y = jnp.einsum('bdn,bn->bd', state, c)
            return (state, y)
        init = jnp.zeros((b, D_INNER, D_STATE), dtype=u.dtype)
        _, ys = jax.lax.scan(step, init, (jnp.transpose(deltaA, (1, 0, 2, 3)), jnp.transpose(deltaB_u, (1, 0, 2, 3)), jnp.transpose(Cm, (1, 0, 2))))
        y = jnp.transpose(ys, (1, 0, 2)) + u * D
        y = y * _silu(res)
        return y @ out_proj_w.T + x_copy

    def _L0_ffn_ref(x, w_gate, w_up, w_down):
        import jax, jax.numpy as jnp
        import numpy as np
        DIM = 128
        HIDDEN = 384
        SCALE = 1.0 / 127.0

        def _dequant(w_int, dtype):
            return w_int.astype(dtype) * jnp.asarray(SCALE, dtype)
        wg = _dequant(w_gate, x.dtype)
        wu = _dequant(w_up, x.dtype)
        wd = _dequant(w_down, x.dtype)
        gate = jnp.einsum('bsd,hd->bsh', x, wg)
        up = jnp.einsum('bsd,hd->bsh', x, wu)
        h = jax.nn.silu(gate) * up
        return jnp.einsum('bsh,dh->bsd', h, wd)
    x = L0_attn_x
    x = _layernorm(x + _L0_attn_ref(x, L0_attn_norm_w, L0_attn_in_proj_w, L0_attn_conv_w, L0_attn_conv_b, L0_attn_x_proj_w, L0_attn_dt_proj_w, L0_attn_dt_proj_b, L0_attn_A_log, L0_attn_D, L0_attn_out_proj_w), axis=-1)
    x = _layernorm(x + _L0_ffn_ref(x, L0_ffn_w_gate, L0_ffn_w_up, L0_ffn_w_down), axis=-1)
    return x

_drawn_inputs = setup_inputs


def setup_inputs(seed=0):
    import zlib

    import numpy as np

    out = dict(_drawn_inputs(seed))
    spreads = {'L0_attn_norm_w': (1.0, 0.6),
     'L0_attn_conv_b': (0.0, 0.8),
     'L0_attn_dt_proj_b': (0.0, 0.8),
     'L0_attn_D': (1.0, 0.6)}
    factors = {'L0_attn_in_proj_w': 8.0,
     'L0_attn_conv_w': 8.0,
     'L0_attn_x_proj_w': 8.0,
     'L0_attn_dt_proj_w': 8.0,
     'L0_attn_A_log': 8.0,
     'L0_attn_out_proj_w': 8.0}
    for name, (base, spread) in spreads.items():
        noise = np.random.default_rng([zlib.crc32(name.encode()), seed]).standard_normal(out[name].shape)
        drawn = base * np.exp(spread * noise) if base else spread * noise
        out[name] = jnp.asarray(drawn.astype(out[name].dtype))
    for name, factor in factors.items():
        out[name] = (out[name] * factor).astype(out[name].dtype)
    return out
```

```python
import concourse.bass as bass
from concourse import mybir
from contextlib import ExitStack


def mamba_swiglu_postln(nc, x, norm_w, in_w, conv_w, conv_b, xp_w, dt_w, dt_b, a_log, d_skip, out_w,
                        gate_w, up_w, down_w, out):
    f32, f32r, i32 = mybir.dt.float32, mybir.dt.float32r, mybir.dt.int32
    ALU, ACT, AX = mybir.AluOpType, mybir.ActivationFunctionType, mybir.AxisListType

    P = 128
    H = P // 2
    B, T, M = x.shape
    TILES = T // P
    DI = out_w.shape[1]
    HALVES = DI // P
    NS = a_log.shape[1]
    R = dt_w.shape[1]
    TAPS = conv_w.shape[2]
    J = P // NS
    GH = P // J
    QUADS = DI // J // 4
    QH = QUADS // HALVES
    GROUPS = 4 * QUADS
    HID = gate_w.shape[0] // P
    XB = R + NS
    WSCALE = 1.0 / 127.0
    SILU2 = WSCALE * WSCALE * WSCALE / 2
    EPS = 1e-5
    RING = 4

    ctx = ExitStack()
    with ctx:
        def sb(name, shape, dt=f32):
            return ctx.enter_context(nc.sbuf_tensor(name, shape, dt))

        def pair(name, shape, dt=f32):
            return [sb(f"{name}{i}", shape, dt) for i in range(2)]

        def pb(name):
            return ctx.enter_context(nc.psum_tensor(name, [P, T], f32))

        def sem(name):
            return ctx.enter_context(nc.semaphore(name))

        in_t = sb("in_t", [M, 2 * HALVES, P])
        xb_t = sb("xb_t", [P, HALVES, XB])
        xc_t = sb("xc_t", [P, HALVES, J, NS])
        dt_t = sb("dt_t", [R, HALVES, P])
        out_t = sb("out_t", [P, HALVES, M])
        gate_t = sb("gate_t", [M, HID, P], f32r)
        up_t = sb("up_t", [M, HID, P], f32r)
        down_t = sb("down_t", [P, HID, M])
        nw = sb("nw", [M, 1])
        cw = sb("cw", [P, HALVES, TAPS])
        cb = sb("cb", [P, HALVES])
        dtb = sb("dtb", [P, HALVES])
        dsk = sb("dsk", [P, HALVES])
        dhalf = sb("dhalf", [P, HALVES])
        a_exp = sb("a_exp", [P, DI // J])
        a_neg = sb("a_neg", [P, DI // J])
        ident = sb("ident", [P, P])
        perm = sb("perm", [P, P])
        spread = sb("spread", [P, GH // 2, P], f32r)
        lane_f = sb("lane_f", [P, J])
        gather = sb("gather", [P, QH, 4 * J])
        powm = sb("powm", [P, B * TILES])
        x_all = sb("x_all", [P, B * TILES, M])
        x_ss = sb("x_ss", [P, B * TILES])
        x_ms = sb("x_ms", [P, B * TILES])
        x_rs = sb("x_rs", [P, B * TILES])
        hx = sb("hx", [P, TILES, M])
        h_t = sb("h_t", [M, T])
        xs = sb("xs", [P, HALVES, TAPS - 1 + T])
        tap = [sb(f"tap{i}", [P, HALVES, T]) for i in range(TAPS)]
        conv = sb("conv", [P, HALVES, T])
        conv_th = sb("conv_th", [P, HALVES, T])
        res_th = sb("res_th", [P, HALVES, T])
        z_abs, z_pos, z_ln, z_w, z_e, z_c, du = tap[1], tap[3], tap[0], tap[2], conv_th, res_th, tap[1]
        xd = sb("xd", [XB, T])
        delta = sb("delta", [P, HALVES, T])
        d_hi = sb("d_hi", [P, HALVES, T], f32r)
        d_lo = sb("d_lo", [P, HALVES, T], f32r)
        u2 = pair("u2_", [P, HALVES, T])
        sres = pair("sres", [P, HALVES, T])
        du_t = pair("du_t", [P, QUADS, TILES, 4 * J])
        b_t = pair("b_t", [P, TILES, NS])
        c_rep = pair("c_rep", [P, T])
        d_pack = pair("d_pack", [P, 2 * HALVES, T], f32r)
        y_out_all = sb("y_out", [P, 2, TILES * M])
        y_out = [y_out_all[:, i, :].rearrange("p (i m) -> p i m", m=M) for i in range(2)]
        prod_all = sb("prod", [P, 2, TILES * 4 * P])
        prod = [prod_all[:, i, :].rearrange("p (i c f) -> p i c f", i=TILES, c=4) for i in range(2)]
        decay = [sb(f"decay{i}", [P, T]) for i in range(RING)]
        state = sb("state", [P, 4, T])
        weighted = pair("weighted", [P, 4, T])
        x_sq = prod_all[:, :, :].rearrange("p a f -> p (a f)")

        def room(buf):
            flat, at = buf[:, :, :].rearrange("p c t -> p (c t)"), [0]

            def cut(rows, cols, dt=f32):
                at[0] += cols
                assert at[0] <= 4 * T
                return flat[0:rows, at[0] - cols:at[0]].bitcast(dt)
            return cut

        cut = room(state)
        in_raw = cut(P, 2 * HALVES * M).rearrange("p (c m) -> p c m", m=M)
        xp_raw, dt_raw = cut(XB + NS, DI), cut(P, HALVES * R).rearrange("p (h r) -> p h r", r=R)
        al_raw, out_raw = cut(DI // J, P), cut(M, DI)
        cut = room(weighted[0])
        gate_raw, up_raw = [cut(P, HID * M, i32).rearrange("p (b m) -> p b m", m=M) for _ in range(2)]
        down_raw = cut(M, HID * P, i32)
        cut = room(weighted[1])
        gate_f, up_f = [cut(P, HID * M).rearrange("p (b m) -> p b m", m=M) for _ in range(2)]
        down_f = cut(M, HID * P)
        spread_f = y_out_all[:, :, :].rearrange("p a f -> p (a f)").rearrange(
            "p (s j n) -> p s j n", j=J, n=NS)
        g = sb("g", [P, HALVES, T])
        r1 = sb("r1", [P, TILES, M])
        st1 = sb("st1", [P, TILES, 6])
        mv1 = sb("mv1", [P, TILES, 2])
        ve1 = sb("ve1", [P, TILES])
        rs1 = sb("rs1", [P, TILES])
        x1 = sb("x1", [P, TILES, M])
        x1_hi = sb("x1_hi", [M, T], f32r)
        x1_lo = sb("x1_lo", [M, T], f32r)
        g_th = sb("g_th", [P, 2, T])
        g_act = sb("g_act", [P, HID, T])
        r2 = sb("r2", [P, TILES, M])
        st2 = sb("st2", [P, TILES, 6])
        mv2 = sb("mv2", [P, TILES, 2])
        ve2 = sb("ve2", [P, TILES])
        rs2 = sb("rs2", [P, TILES])

        delta_ps = [pb(f"delta_ps{i}") for i in range(2)]
        drive_ps = [pb(f"drive_ps{i}") for i in range(2)]
        y_ps = [pb(f"y_ps{i}") for i in range(HALVES)]
        dense_ps = [pb(f"dense_ps{i}") for i in range(2)]

        ld_x0 = sem("ld_x0")
        ld_x = sem("ld_x")
        ld_in = sem("ld_in")
        ld_xp = sem("ld_xp")
        ld_vec = sem("ld_vec")
        ld_out = sem("ld_out")
        ld_ffn = sem("ld_ffn")
        consts0 = sem("consts0")
        consts = sem("consts")
        consts_dve = sem("consts_dve")
        spread_ready = sem("spread_ready")
        wt_turned = sem("wt_turned")
        wt_taken = sem("wt_taken")
        ffn_float = sem("ffn_float")
        a_exped = sem("a_exped")
        a_ready = sem("a_ready")
        sq_ready = sem("sq_ready")
        ms_step = sem("ms_step")
        ms_ready = sem("ms_ready")
        rs_ready = sem("rs_ready")
        hx_ready = sem("hx_ready")
        full = [sem(f"full{i}") for i in range(2)]
        taken = [sem(f"taken{i}") for i in range(2)]
        taps_ready = sem("taps_ready")
        conv_part = sem("conv_part")
        conv_ready = sem("conv_ready")
        conv_th_ready = sem("conv_th_ready")
        res_th_ready = sem("res_th_ready")
        u2_ready = sem("u2_ready")
        z_step = sem("z_step")
        z_ln_ready = sem("z_ln_ready")
        soft_step = sem("soft_step")
        delta_ready = sem("delta_ready")
        du_ready = sem("du_ready")
        hi_ready = sem("hi_ready")
        lo_ready = sem("lo_ready")
        packed = sem("packed")
        delta_spread = sem("delta_spread")
        decay_ready = sem("decay_ready")
        prod_ready = sem("prod_ready")
        drive_ready = sem("drive_ready")
        scanned = sem("scanned")
        weighted_ready = sem("weighted_ready")
        summed = sem("summed")
        y_taken = sem("y_taken")
        g_ready = sem("g_ready")
        r1_ready = sem("r1_ready")
        ln1_step = sem("ln1_step")
        ve1_ready = sem("ve1_ready")
        rs1_ready = sem("rs1_ready")
        x1_ready = sem("x1_ready")
        x1_hi_ready = sem("x1_hi_ready")
        g_th_ready = sem("g_th_ready")
        g_act_ready = sem("g_act_ready")
        r2_ready = sem("r2_ready")
        ln2_step = sem("ln2_step")
        ve2_ready = sem("ve2_ready")
        rs2_ready = sem("rs2_ready")
        y_ready = sem("y_ready")
        y_free = [sem(f"y_free{i}") for i in range(2)]

        IN_JOBS = [(1, "h"), (3, "xs0"), (4, "xs1"), (9, "res0"), (10, "res1"), (18, "xd"), (19, "crep"),
                   (20, "z0"), (21, "z1"), (22, "bt"), (30, "dut0"), (31, "dut1")]
        OUT_JOBS = [(6, "proj"), (15, "x1"), (20, "gate0"), (21, "up0"), (23, "gate1"), (24, "up1"),
                    (26, "gate2"), (27, "up2"), (28, "down0"), (29, "down1")]
        ALL_JOBS = sorted(IN_JOBS + OUT_JOBS, key=lambda job: job[0])

        def jobs_of(k):
            return [n for _, n in (IN_JOBS if k < 1 else OUT_JOBS if k > B - 2 else ALL_JOBS)]

        class Iteration:

            def __init__(self, k0, ahead=0):
                self.k0, self.ahead = k0, ahead
                self.scan = 0 <= k0 < B
                self.ins = k0 < B - 1
                self.outs = k0 > 0
                self.now, self.next = k0 % 2, (k0 + 1) % 2
                self.names = jobs_of(k0)
                self.before = sum(len(jobs_of(k)) for k in range(-1, k0))

            def count(self, each, batch, n):
                return each * (self.k0 + batch) + n + each * self.ahead

            def wait(self, eng, s, each, batch, n):
                if each * (self.k0 + batch) + n > 0:
                    eng.wait_ge(s, self.count(each, batch, n))

            def bank(self, name):
                return (self.before + self.names.index(name)) % 2

            def job_count(self, name, less=0):
                at = (self.before + self.names.index(name)) // 2 + 1 - less
                return at, at + len(ALL_JOBS) // 2 * self.ahead

            def wait_full(self, eng, name):
                eng.wait_ge(full[self.bank(name)], self.job_count(name)[1])

            def wait_taken(self, eng, name):
                eng.wait_ge(taken[self.bank(name)], self.job_count(name)[1])

            def wait_free(self, eng, name):
                at, value = self.job_count(name, 1)
                if at > 0:
                    eng.wait_ge(taken[self.bank(name)], value)

            def ps(self, name):
                return dense_ps[self.bank(name)]

            def take(self, ins, name):
                ins.then_inc(taken[self.bank(name)], 1)

        def run(eng, iteration):
            for k in (-1, 0):
                iteration(Iteration(k))
            with eng.Fori(0, (B - 2) // 2) as i:
                for k in (1, 2):
                    iteration(Iteration(k, 2 * i))
            for k in (B - 1, B):
                iteration(Iteration(k))

        block = ctx.enter_context(nc.Block())

        @block.sync
        def _(sp):
            for s in y_free:
                sp.sem_inc(s, 16)
            xv = x.rearrange("b (i t) m -> t (b i) m", t=P)
            sp.dma_start(x_all[:, 0:TILES, :], xv[:, 0:TILES, :]).then_inc(ld_x0, 16)
            sp.dma_start(xp_raw[:, :], xp_w).then_inc(ld_xp, 16)
            sp.dma_start(dt_raw[:, :, :], dt_w.rearrange("(h d) r -> d h r", h=HALVES)).then_inc(ld_xp, 16)
            sp.dma_start(x_all[:, TILES:, :], xv[:, TILES:, :]).then_inc(ld_x, 16)
            sp.dma_start(gate_raw[:, :, :], gate_w.rearrange("(b h) m -> h b m", h=P)).then_inc(ld_ffn, 16)
            sp.dma_start(up_raw[:, :, :], up_w.rearrange("(b h) m -> h b m", h=P)).then_inc(ld_ffn, 16)
            sp.dma_start(down_raw[:, :], down_w).then_inc(ld_ffn, 16)

            y_rows = out.rearrange("b t m -> (b t) m")

            def iteration(it):
                def value(v):
                    return v if isinstance(v, int) else sp.snap(v)

                both, done, row = value(it.count(1, 1, 1)), value(it.count(1, -1, 1)), value((it.k0 - 1 + it.ahead) * T)
                if it.ins:
                    sp.wait_ge(hi_ready, both)
                    sp.wait_ge(lo_ready, both)
                    for part, src in enumerate((d_hi, d_lo)):
                        for h in range(HALVES):
                            for half in range(2):
                                sp.dma_start(d_pack[it.next][H * part:H * part + H, 2 * h + half, :].bitcast(f32),
                                             src[H * half:H * half + H, h, :].bitcast(f32)).then_inc(packed, 16)
                if it.outs:
                    rows = y_rows[row:row + T, :] if isinstance(row, int) else y_rows[bass.ds(row, T), :]
                    sp.wait_ge(y_ready, done)
                    sp.dma_start(rows.rearrange("(i t) m -> t i m", t=P), y_out[it.next][:, :, :]
                                 ).then_inc(y_free[it.next], 16)

            run(sp, iteration)
            for s in y_free:
                sp.wait_ge(s, 16 + 16 * (B // 2))

        @block.tensor
        def _(pe):
            mm, turn = pe.matmul, pe.transpose
            pe.wait_ge(consts, 1)
            pe.wait_ge(ld_in, 16)
            for c in range(2 * HALVES):
                last = turn(delta_ps[0][:, c * P:(c + 1) * P], in_raw[:, c, :], ident[:, :])
            last.then_inc(wt_turned, 1)
            pe.wait_ge(ld_xp, 32)
            for h in range(HALVES):
                turn(delta_ps[1][:, h * P:h * P + XB + NS], xp_raw[:, h * P:(h + 1) * P],
                     ident[0:XB + NS, 0:XB + NS])
                last = turn(delta_ps[1][0:R, (2 + h) * P:(3 + h) * P], dt_raw[:, h, :], ident[:, :])
            last.then_inc(wt_turned, 1)
            pe.wait_ge(ld_out, 32)
            turn(drive_ps[0][:, 0:DI // J], al_raw[:, :], ident[0:DI // J, 0:DI // J])
            for h in range(HALVES):
                last = turn(drive_ps[0][:, (1 + h) * P:(2 + h) * P], out_raw[:, h * P:(h + 1) * P], ident[:, :])
            last.then_inc(wt_turned, 1)

            def ffn_weights():
                pe.wait_ge(ffn_float, 3)
                for ps, w in ((drive_ps[1], lambda b: gate_f[:, b, :]), (y_ps[0], lambda b: up_f[:, b, :]),
                              (y_ps[1], lambda b: down_f[:, b * P:(b + 1) * P])):
                    for b in range(HID):
                        last = turn(ps[:, b * P:(b + 1) * P], w(b), ident[:, :])
                    last.then_inc(wt_turned, 1)

            def spread_delta(it, n, batch=0):
                side = it.now if batch == 0 else it.next
                h, q, c = n // 4 // QH, n // 4 % QH, n % 4
                gl = 4 * c + q
                if n == 0:
                    it.wait(pe, packed, 16 * 4 * HALVES, batch, 16 * 4 * HALVES)
                it.wait(pe, decay_ready, GROUPS, batch, n - 1)
                mm(delta_ps[n % 2][:, :], spread[:, gl % J, :], d_pack[side][:, 2 * h + gl // J, :],
                   start=True, stop=True).then_inc(delta_spread, 1)

            def turn_drive(it, n):
                quad, c = n // 4, n % 4
                if c == 0:
                    it.wait(pe, prod_ready, QUADS, 0, quad + 1)
                it.wait(pe, scanned, GROUPS, 0, n - 1)
                for i in range(TILES):
                    last = turn(drive_ps[n % 2][:, i * P:(i + 1) * P], prod[quad % 2][:, i, c, :], ident[:, :])
                last.then_inc(drive_ready, 1)

            def sum_states(it, quad, batch=0):
                h, q = quad // QH, quad % QH
                it.wait(pe, weighted_ready, QUADS, batch, quad + 1)
                if q == 0:
                    it.wait(pe, y_taken, HALVES, batch - 1, h + 1)
                for c in range(4):
                    last = mm(y_ps[h][32 * c:32 * c + 32, :], gather[:, q, :], weighted[quad % 2][:, c, :],
                              start=(q == 0), stop=(q == QH - 1), tile_position=(0, 32 * c))
                last.then_inc(summed, 1)

            def job(it, name):
                ps, kind, n = it.ps(name), name.rstrip("0123456789"), int(name[-1]) if name[-1].isdigit() else 0
                if name == "x1":
                    kind, n = "x1", 0
                it.wait_free(pe, name)
                if kind == "h":
                    it.wait(pe, hx_ready, 1, 1, 1)
                    for i in range(TILES):
                        last = turn(ps[:, i * P:(i + 1) * P], hx[:, i, :], ident[:, :])
                elif kind in ("xs", "res"):
                    if kind == "xs" and n == 0:
                        it.wait_taken(pe, "h")
                    last = mm(ps[:, :], in_t[:, n + (HALVES if kind == "res" else 0), :], h_t[:, :],
                              start=True, stop=True)
                elif kind in ("xd", "crep"):
                    it.wait(pe, u2_ready, 1, 1, 1)
                    for h in range(HALVES):
                        w = xb_t[:, h, :] if kind == "xd" else xc_t[:, h, :, :].rearrange("p j n -> p (j n)")
                        last = mm(ps[0:XB if kind == "xd" else P, :], w, u2[it.next][:, h, :],
                                  start=(h == 0), stop=(h == HALVES - 1))
                elif kind == "z":
                    it.wait_taken(pe, "xd")
                    last = mm(ps[:, :], dt_t[:, n, :], xd[0:R, :], start=True, stop=True)
                elif kind == "bt":
                    for i in range(TILES):
                        last = turn(ps[:, i * XB:(i + 1) * XB], xd[:, i * P:(i + 1) * P], ident[0:XB, 0:XB])
                elif kind == "dut":
                    it.wait(pe, du_ready, 1, 1, 1)
                    for i in range(2):
                        for h in range(HALVES):
                            last = turn(ps[:, (i * HALVES + h) * P:(i * HALVES + h + 1) * P],
                                        du[:, h, (2 * n + i) * P:(2 * n + i + 1) * P], perm[:, :])
                elif kind == "proj":
                    it.wait(pe, g_ready, HALVES, -1, HALVES)
                    for i in range(TILES):
                        for h in range(HALVES):
                            last = mm(ps[:, i * P:(i + 1) * P], g[:, h, i * P:(i + 1) * P],
                                      out_t[:, h, :], start=(h == 0), stop=(h == HALVES - 1))
                elif kind == "x1":
                    it.wait(pe, x1_ready, 1, -1, 1)
                    for i in range(TILES):
                        last = turn(ps[:, i * P:(i + 1) * P], x1[:, i, :], ident[:, :])
                elif kind in ("gate", "up"):
                    if name == "gate0":
                        it.wait(pe, x1_hi_ready, 1, -1, 1)
                        it.wait_taken(pe, "x1")
                    w = (gate_t if kind == "gate" else up_t)[:, n, :]
                    mm(ps[:, :], w, x1_hi[:, :], start=True, stop=False)
                    last = mm(ps[:, :], w, x1_lo[:, :], start=False, stop=True)
                elif kind == "down":
                    it.wait_taken(pe, f"up{HID - 1}")
                    for i in range(2):
                        for b in range(HID):
                            last = mm(ps[:, i * P:(i + 1) * P], g_act[:, b, (2 * n + i) * P:(2 * n + i + 1) * P],
                                      down_t[:, b, :], start=(b == 0), stop=(b == HID - 1))
                last.then_inc(full[it.bank(name)], 1)

            def iteration(it):
                todo = list(it.names)
                when = dict((n, s) for s, n in ALL_JOBS)
                if it.k0 == -1:
                    pe.wait_ge(wt_taken, 3)
                for n in range(GROUPS):
                    if it.scan:
                        if n + 1 < GROUPS:
                            spread_delta(it, n + 1)
                        turn_drive(it, n)
                        if n % 4 == 1 and (n > 1 or it.k0 > 0):
                            if n > 1:
                                sum_states(it, n // 4 - 1)
                            else:
                                sum_states(it, QUADS - 1, -1)
                    elif n == 1 and it.k0 == B:
                        sum_states(it, QUADS - 1, -1)
                    while todo and when[todo[0]] <= n:
                        job(it, todo.pop(0))
                if it.ins:
                    if it.k0 == -1:
                        ffn_weights()
                        pe.wait_ge(wt_taken, 6)
                        pe.wait_ge(spread_ready, 1)
                    spread_delta(it, 0, 1)

            run(pe, iteration)

        @block.scalar
        def _(act):
            A = act.activation
            act.dma_start(in_raw[:, :, :], in_w.rearrange("(c d) m -> d c m", d=P)).then_inc(ld_in, 16)
            act.dma_start(nw[:, :], norm_w.rearrange("(m o) -> m o", o=1)).then_inc(ld_vec, 16)
            act.dma_start(cw[:, :, :], conv_w.rearrange("(h d) o j -> d h (o j)", h=HALVES)).then_inc(ld_vec, 16)
            with nc.allow_non_contiguous_dma(reason="a few vectors, once"):
                for dst, src in ((cb, conv_b), (dtb, dt_b), (dsk, d_skip)):
                    act.dma_start(dst[:, :], src.rearrange("(h d) -> d h", h=HALVES)).then_inc(ld_vec, 16)
            act.dma_start(al_raw[:, :], a_log.rearrange("(g j) n -> g (j n)", j=J)).then_inc(ld_out, 16)
            act.dma_start(out_raw[:, :], out_w).then_inc(ld_out, 16)
            act.wait_ge(ld_x0, 16)
            flat = x_all[:, :, :].rearrange("p b m -> p (b m)")
            first = TILES * M
            A(x_sq[:, 0:first], flat[:, 0:first], ACT.Square).then_inc(sq_ready, 1)
            act.wait_ge(ld_vec, 16 * 5)

            def late_setup():
                act.wait_ge(wt_turned, 3)
                A(a_exp[:, :], drive_ps[0][:, 0:DI // J], ACT.Exp).then_inc(a_exped, 1)
                act.wait_ge(consts, 1)
                A(spread[:, :, :], spread_f[:, :, :, :].rearrange("p s j n -> p s (j n)"), ACT.Copy
                  ).then_inc(spread_ready, 1)
                act.wait_ge(ld_x, 16)
                A(x_sq[:, first:], flat[:, first:], ACT.Square).then_inc(sq_ready, 1)
                act.wait_ge(a_ready, 1)

            def exp_decay(it, n):
                h, q, c = n // 4 // QH, n // 4 % QH, n % 4
                it.wait(act, delta_spread, GROUPS, 0, n + 1)
                it.wait(act, scanned, GROUPS, 0, n + 1 - RING)
                col = GH * h + 4 * c + q
                A(decay[n % RING][:, :], delta_ps[n % 2][:, :], ACT.Exp, scale=a_neg[:, col:col + 1]
                  ).then_inc(decay_ready, 1)

            def dense(it, step):
                if it.ins:
                    if step == 2:
                        it.wait_full(act, "h")
                        it.take(A(h_t[:, :], it.ps("h")[:, :], ACT.Copy, scale=nw[:, 0:1]), "h")
                    if step in (4, 5):
                        name = f"xs{step - 4}"
                        it.wait_full(act, name)
                        if step == 4:
                            it.wait(act, conv_ready, 1, 0, 1)
                        it.take(A(xs[:, step - 4, TAPS - 1:], it.ps(name)[:, :], ACT.Copy), name)
                    if 5 <= step < 9:
                        h = (step - 5) // 2
                        if step % 2:
                            it.wait_taken(act, f"xs{h}")
                            if step == 5 and it.k0 == -1:
                                act.wait_ge(consts_dve, 1)
                        for j in range(2 * (1 - step % 2), 2 * (1 - step % 2) + 2):
                            A(tap[j][:, h, :], xs[:, h, j:j + T], ACT.Identity, scale=cw[:, h, j:j + 1],
                              bias=cb[:, h:h + 1] if j == 0 else 0.0).then_inc(taps_ready, 1)
                    if step in (10, 11):
                        name = f"res{step - 10}"
                        it.wait_full(act, name)
                        A(res_th[:, step - 10, :], it.ps(name)[:, :], ACT.Tanh, scale=0.5).then_inc(res_th_ready, 1)
                    if step == 17:
                        it.wait(act, conv_ready, 1, 1, 1)
                        A(conv_th[:, :, :], conv[:, :, :], ACT.Tanh, scale=0.5).then_inc(conv_th_ready, 1)
                    if step == 19:
                        it.wait_full(act, "xd")
                        it.take(A(xd[:, :], it.ps("xd")[0:XB, :], ACT.Copy), "xd")
                    if step == 20:
                        it.wait_full(act, "crep")
                        it.take(A(c_rep[it.next][:, :], it.ps("crep")[:, :], ACT.Copy), "crep")
                    if step in (21, 22):
                        h, name = step - 21, f"z{step - 21}"
                        it.wait_full(act, name)
                        A(z_abs[:, h, :], it.ps(name)[:, :], ACT.Abs, bias=dtb[:, h:h + 1]).then_inc(z_step, 1)
                        it.take(A(z_pos[:, h, :], it.ps(name)[:, :], ACT.Relu, bias=dtb[:, h:h + 1]), name)
                    if step == 22:
                        it.wait(act, z_step, 3, 1, 2)
                        A(z_e[:, :, :], z_abs[:, :, :], ACT.Exp, scale=-1.0).then_inc(z_step, 1)
                        it.wait(act, z_step, 3, 1, 3)
                        A(z_ln[:, :, :], z_e[:, :, :], ACT.Ln, bias=1.0).then_inc(z_ln_ready, 1)
                        it.wait_full(act, "bt")
                        it.take(A(b_t[it.next][:, :, :],
                                  it.ps("bt")[:, 0:TILES * XB].rearrange("p (i r) -> p i r", i=TILES)[:, :, R:XB],
                                  ACT.Copy), "bt")
                    if step == 27:
                        it.wait(act, delta_ready, 1, 1, 1)
                        A(d_hi[:, :, :], delta[:, :, :], ACT.Copy).then_inc(hi_ready, 1)
                    if step == 31:
                        for n in range(2):
                            name = f"dut{n}"
                            it.wait_full(act, name)
                            dst = du_t[it.next][:, :, 2 * n:2 * n + 2, :]
                            src = it.ps(name)[:, :].rearrange("p (i e f) -> p e i f", i=2, f=4 * J)
                            it.take(A(dst, src, ACT.Copy), name)
                if it.outs:
                    if step == 16:
                        it.wait_full(act, "x1")
                        A(x1_hi[:, :], it.ps("x1")[:, :], ACT.Copy).then_inc(x1_hi_ready, 1)
                    for b, at in enumerate((21, 24, 27)):
                        if step == at:
                            it.wait_full(act, f"gate{b}")
                            A(g_th[:, b % 2, :], it.ps(f"gate{b}")[:, :], ACT.Tanh, scale=WSCALE / 2
                              ).then_inc(g_th_ready, 1)

            def iteration(it):
                for n in range(GROUPS):
                    if it.scan:
                        exp_decay(it, n)
                    dense(it, n)
                if it.k0 == -1:
                    late_setup()

            run(act, iteration)

        @block.gpsimd
        def _(pool):
            TT = pool.tensor_tensor
            for t in (ident, perm, spread_f):
                pool.memset(t[:], 0.0).then_inc(consts0, 1)
            pool.memset(lane_f[:, :], 1.0).then_inc(consts0, 1)
            pool.memset(powm[:, :], -0.5).then_inc(consts0, 1)
            pool.wait_ge(consts0, 5)
            sel = pool.affine_select
            sel(out=ident[:, :], in_=ident[:, :], compare_op=ALU.not_equal, fill=1.0, base=0,
                pattern=[[-1, P]], channel_multiplier=1)
            sel(out=perm[:, :], in_=perm[:, :], compare_op=ALU.not_equal, fill=1.0, base=0,
                pattern=[[-J, 4], [-4 * J, 4], [-1, J]], channel_multiplier=1)
            sel(out=lane_f[:, :], in_=lane_f[:, :], compare_op=ALU.is_ge, fill=0.0, base=0,
                pattern=[[-NS, J]], channel_multiplier=1).then_inc(consts0, 1)
            pool.wait_ge(consts0, 6)
            sel(out=lane_f[:, :], in_=lane_f[:, :], compare_op=ALU.is_ge, fill=0.0, base=NS - 1,
                pattern=[[NS, J]], channel_multiplier=-1)
            sel(out=spread_f[:], in_=spread_f[:], compare_op=ALU.not_equal, fill=1.0, base=0,
                pattern=[[-J, GH // 2], [-1, J], [0, NS]], channel_multiplier=1).then_inc(consts0, 1)
            pool.wait_ge(consts0, 7)
            sel(out=spread_f[:], in_=spread_f[:], compare_op=ALU.not_equal, fill=1.0, base=-H,
                pattern=[[-J, GH // 2], [-1, J], [0, NS]], channel_multiplier=1).then_inc(consts, 1)
            pool.wait_ge(ms_ready, 1)
            TT(x_rs[:, 0:TILES], x_ms[:, 0:TILES], powm[:, 0:TILES], ALU.pow).then_inc(rs_ready, 1)
            pool.wait_ge(rs_ready, 1)

            def scale_x(it):
                if it.k0 >= 0:
                    at, value = it.k0, it.k0 + it.ahead
                    wait_h(it)
                lo = (it.k0 + 1 + it.ahead) * TILES
                xk = x_all[:, bass.ds(lo, TILES), :] if not isinstance(lo, int) else x_all[:, lo:lo + TILES, :]
                rk = x_rs[:, bass.ds(lo, TILES)] if not isinstance(lo, int) else x_rs[:, lo:lo + TILES]
                TT(hx[:, :, :], xk, rk.unsqueeze(2).broadcast_to([P, TILES, M]), ALU.mult).then_inc(hx_ready, 1)

            def wait_h(it):
                it.wait(pool, u2_ready, 1, 0, 1)

            def multiply(it, quad):
                if quad == 0:
                    pool_wait_in(it)
                it.wait(pool, drive_ready, GROUPS, 0, 4 * (quad - 1))
                a = du_t[it.now][:, quad, :, :].unsqueeze(3).broadcast_to([P, TILES, 4 * J, NS])
                b = b_t[it.now][:, :, :].unsqueeze(2).broadcast_to([P, TILES, 4 * J, NS])
                o = prod[quad % 2][:, :, :, :].rearrange("p i c (j n) -> p i (c j) n", n=NS)
                TT(o, a, b, ALU.mult).then_inc(prod_ready, 1)

            def pool_wait_in(it):
                prev = Iteration(it.k0 - 1, it.ahead)
                for name in ("dut0", "dut1"):
                    prev.wait_taken(pool, name)

            def iteration(it):
                if it.ins:
                    scale_x(it)
                for quad in range(QUADS):
                    if it.scan:
                        multiply(it, quad)
                    if it.ins and quad == 3:
                        it.wait(pool, taps_ready, HALVES * TAPS, 1, HALVES * TAPS)
                        it.wait(pool, u2_ready, 1, 0, 1)
                        TT(tap[0][:], tap[0][:], tap[1][:], ALU.add).then_inc(conv_part, 1)
                        TT(tap[2][:], tap[2][:], tap[3][:], ALU.add).then_inc(conv_part, 1)
                    if it.outs and quad == 3:
                        it.wait(pool, ve1_ready, 1, -1, 1)
                        TT(rs1[:, :], ve1[:, :], powm[:, 0:TILES], ALU.pow).then_inc(rs1_ready, 1)
                    if it.ins and quad == 4:
                        it.wait(pool, conv_part, 2, 1, 2)
                        TT(conv[:], tap[0][:], tap[2][:], ALU.add).then_inc(conv_ready, 1)
                    if it.ins and quad == 7:
                        it.wait(pool, hi_ready, 1, 1, 1)
                        it.wait(pool, packed, 16 * 4 * HALVES, 0, 16 * 4 * HALVES)
                        TT(d_lo[:], delta[:], d_hi[:].bitcast(f32), ALU.subtract).then_inc(lo_ready, 1)
                    if it.outs and quad == 7:
                        it.wait(pool, ve2_ready, 1, -1, 1)
                        TT(rs2[:, :], ve2[:, :], powm[:, 0:TILES], ALU.pow).then_inc(rs2_ready, 1)
                if it.k0 == -1:
                    pool.wait_ge(ld_ffn, 48)
                    pool.tensor_copy(gate_f[:], gate_raw[:]).then_inc(ffn_float, 1)
                    pool.tensor_copy(up_f[:], up_raw[:]).then_inc(ffn_float, 1)
                    pool.tensor_copy(down_f[:], down_raw[:]).then_inc(ffn_float, 1)
                    pool.wait_ge(ms_ready, 2)
                    TT(x_rs[:, TILES:], x_ms[:, TILES:], powm[:, TILES:], ALU.pow).then_inc(rs_ready, 1)
                    pool.wait_ge(rs_ready, 2)

            run(pool, iteration)

        @block.vector
        def _(dve):
            TT, TS, STT = dve.tensor_tensor, dve.tensor_scalar, dve.scalar_tensor_tensor

            def mean_square(n, lo, hi):
                dve.wait_ge(sq_ready, n)
                dve.tensor_reduce(out=x_ss[:, lo:hi], in_=x_sq[:, lo * M:hi * M].rearrange("p (t m) -> p t m", m=M),
                                  op=ALU.add, axis=AX.X).then_inc(ms_step, 1)
                dve.wait_ge(ms_step, n)
                TS(x_ms[:, lo:hi], x_ss[:, lo:hi], 1.0 / M, EPS, ALU.mult, ALU.add).then_inc(ms_ready, 1)

            dve.memset(xs[:, :, 0:TAPS - 1], 0.0).then_inc(consts_dve, 1)
            dve.memset(gather[:, :, :], 0.0).then_inc(consts_dve, 1)
            mean_square(1, 0, TILES)
            dve.wait_ge(wt_turned, 1)
            dve.tensor_copy(in_t[:, :, :].rearrange("p c d -> p (c d)"), delta_ps[0][:, :]).then_inc(wt_taken, 1)
            dve.wait_ge(wt_turned, 2)
            wx = delta_ps[1][:, 0:HALVES * P].rearrange("p (h r) -> p h r", h=HALVES)
            TS(xb_t[:, :, 0:R], wx[:, :, 0:R], 0.5, None, ALU.mult)
            TS(xb_t[:, :, R:XB], wx[:, :, R:XB], 0.25, None, ALU.mult)
            for h in range(HALVES):
                TS(xc_t[:, h, :, :], wx[:, h, XB:XB + NS].unsqueeze(1).broadcast_to([P, J, NS]), 0.5, None, ALU.mult)
            dve.tensor_copy(dt_t[:, :, :], delta_ps[1][0:R, HALVES * P:2 * HALVES * P].rearrange(
                "p (h d) -> p h d", h=HALVES)).then_inc(wt_taken, 1)
            dve.wait_ge(wt_turned, 3)
            TS(out_t[:, :, :], drive_ps[0][:, P:(1 + HALVES) * P].rearrange("p (h m) -> p h m", h=HALVES),
               0.5, None, ALU.mult).then_inc(wt_taken, 1)
            dve.wait_ge(ld_vec, 16 * 5)
            TS(dhalf[:, :], dsk[:, :], 0.5, None, ALU.mult)
            dve.wait_ge(consts, 1)
            dve.wait_ge(consts_dve, 2)
            for q in range(QH):
                dve.tensor_copy(gather[:, q, q * J:(q + 1) * J], lane_f[:, :]).then_inc(consts_dve, 1)

            def late_setup():
                dve.wait_ge(a_exped, 1)
                TS(a_neg[:, :], a_exp[:, :], -1.0, None, ALU.mult).then_inc(a_ready, 1)
                mean_square(2, TILES, B * TILES)
                for n, (dst, ps) in enumerate(((gate_t, drive_ps[1]), (up_t, y_ps[0]), (down_t, y_ps[1]))):
                    dve.wait_ge(wt_turned, 4 + n)
                    dve.tensor_copy(dst[:, :, :].rearrange("p b h -> p (b h)"), ps[:, 0:HID * P]
                                    ).then_inc(wt_taken, 1)

            def scan(it, n):
                it.wait(dve, weighted_ready, QUADS, 0, n // 4)
                it.wait(dve, decay_ready, GROUPS, 0, n + 1)
                it.wait(dve, drive_ready, GROUPS, 0, n + 1)
                dve.tensor_tensor_scan(state[:, n % 4, :], decay[n % RING][:, :], drive_ps[n % 2][:, :], 0.0,
                                       ALU.mult, ALU.add).then_inc(scanned, 1)

            def weigh(it, quad):
                it.wait(dve, scanned, GROUPS, 0, 4 * quad + 4)
                it.wait(dve, summed, QUADS, 0, quad - 1)
                if quad == 0:
                    prev = Iteration(it.k0 - 1, it.ahead)
                    prev.wait_taken(dve, "crep")
                TT(weighted[quad % 2][:, :, :], state[:, :, :],
                   c_rep[it.now][:, :].unsqueeze(1).broadcast_to([P, 4, T]), ALU.mult).then_inc(weighted_ready, 1)

            def combine(it, h, batch):
                side = it.now if batch == 0 else it.next
                it.wait(dve, summed, QUADS, batch, QH * (h + 1))
                STT(out=g[:, h, :], in0=u2[side][:, h, :], scalar=dhalf[:, h:h + 1], in1=y_ps[h][:, :],
                    op0=ALU.mult, op1=ALU.add).then_inc(y_taken, 1)
                it.wait(dve, y_taken, HALVES, batch, h + 1)
                TT(g[:, h, :], g[:, h, :], sres[side][:, h, :], ALU.mult).then_inc(g_ready, 1)

            def normalise(it, dst, r, mv, rs, rs_ready_, ready):
                it.wait(dve, rs_ready_, 1, -1, 1)
                for i in range(TILES):
                    last = TS(dst[:, i, :], r[:, i, :], mv[:, i, 0:1], rs[:, i:i + 1], ALU.subtract, ALU.mult)
                last.then_inc(ready, 1)

            def dense(it, step):
                if it.outs:
                    if step == 2:
                        combine(it, 1, -1)
                    if step == 7:
                        it.wait_full(dve, "proj")
                        lo = (it.k0 - 1 + it.ahead) * TILES
                        xk = x_all[:, lo:lo + TILES, :] if isinstance(lo, int) else x_all[:, bass.ds(lo, TILES), :]
                        it.take(STT(out=r1[:, :, :], in0=xk, scalar=2.0,
                                    in1=it.ps("proj")[:, :].rearrange("p (i m) -> p i m", m=M),
                                    op0=ALU.mult, op1=ALU.add), "proj")
                        it.wait_taken(dve, "proj")
                        for i in range(TILES):
                            last = dve.bn_stats(st1[:, i, :], r1[:, i, :])
                        last.then_inc(ln1_step, 1)
                    if step == 8:
                        for i in range(TILES):
                            last = dve.bn_aggr(mv1[:, i, :], st1[:, i, :])
                        last.then_inc(ln1_step, 1)
                        it.wait(dve, ln1_step, 2, -1, 2)
                        TS(ve1[:, :], mv1[:, :, 1], EPS, None, ALU.add).then_inc(ve1_ready, 1)
                    if step == 14:
                        normalise(it, x1, r1, mv1, rs1, rs1_ready, x1_ready)
                if it.ins:
                    if step in (11, 12):
                        h, name = step - 11, f"res{step - 11}"
                        it.wait(dve, res_th_ready, 2, 1, h + 1)
                        it.take(STT(out=sres[it.next][:, h, :], in0=res_th[:, h, :], scalar=1.0,
                                    in1=it.ps(name)[:, :], op0=ALU.add, op1=ALU.mult), name)
                if it.outs and step == 16:
                    it.wait(dve, x1_hi_ready, 1, -1, 1)
                    it.take(TT(x1_lo[:, :], it.ps("x1")[:, :], x1_hi[:, :].bitcast(f32), ALU.subtract), "x1")
                if it.ins and step == 17:
                    it.wait(dve, conv_th_ready, 1, 1, 1)
                    STT(out=u2[it.next][:, :, :], in0=conv_th[:, :, :], scalar=1.0, in1=conv[:, :, :],
                        op0=ALU.add, op1=ALU.mult).then_inc(u2_ready, 1)
                if it.scan and step == 19:
                    combine(it, 0, 0)
                if it.outs:
                    for b, at in enumerate((21, 24, 27)):
                        if step == at:
                            it.wait(dve, g_th_ready, HID, -1, b + 1)
                            it.take(STT(out=g_act[:, b, :], in0=g_th[:, b % 2, :], scalar=1.0,
                                        in1=it.ps(f"gate{b}")[:, :], op0=ALU.add, op1=ALU.mult), f"gate{b}")
                        if step == at + 1:
                            it.wait_full(dve, f"up{b}")
                            it.wait_taken(dve, f"gate{b}")
                            it.take(TT(g_act[:, b, :], g_act[:, b, :], it.ps(f"up{b}")[:, :], ALU.mult), f"up{b}")
                if it.ins and step == 24:
                    it.wait(dve, z_step, 3, 1, 3)
                    TS(z_w[:], z_e[:], 1.0, -1.0, ALU.add, ALU.add).then_inc(soft_step, 1)
                    it.wait(dve, soft_step, 3, 1, 1)
                    TT(z_c[:], z_e[:], z_w[:], ALU.subtract).then_inc(soft_step, 1)
                if it.ins and step == 26:
                    it.wait(dve, z_ln_ready, 1, 1, 1)
                    it.wait_taken(dve, "z1")
                    it.wait(dve, soft_step, 3, 1, 2)
                    TT(z_w[:], z_ln[:], z_c[:], ALU.add).then_inc(soft_step, 1)
                    it.wait(dve, soft_step, 3, 1, 3)
                    TT(delta[:], z_w[:], z_pos[:], ALU.add).then_inc(delta_ready, 1)
                    it.wait(dve, delta_ready, 1, 1, 1)
                    TT(du[:], delta[:], u2[it.next][:], ALU.mult).then_inc(du_ready, 1)
                if it.outs:
                    if step == 29:
                        for n in range(2):
                            it.wait_full(dve, f"down{n}")
                            it.take(STT(out=r2[:, 2 * n:2 * n + 2, :],
                                        in0=it.ps(f"down{n}")[:, 0:2 * M].rearrange("p (i m) -> p i m", m=M),
                                        scalar=SILU2, in1=x1[:, 2 * n:2 * n + 2, :],
                                        op0=ALU.mult, op1=ALU.add), f"down{n}")
                        for n in range(2):
                            it.wait_taken(dve, f"down{n}")
                        for i in range(TILES):
                            last = dve.bn_stats(st2[:, i, :], r2[:, i, :])
                        last.then_inc(ln2_step, 1)
                    if step == 30:
                        for i in range(TILES):
                            last = dve.bn_aggr(mv2[:, i, :], st2[:, i, :])
                        last.then_inc(ln2_step, 1)
                        it.wait(dve, ln2_step, 2, -1, 2)
                        TS(ve2[:, :], mv2[:, :, 1], EPS, None, ALU.add).then_inc(ve2_ready, 1)
                    if step == 31:
                        dve.wait_ge(y_free[it.next], 16 + 16 * ((it.k0 - 1) // 2) + 8 * it.ahead)
                        normalise(it, y_out[it.next], r2, mv2, rs2, rs2_ready, y_ready)

            def iteration(it):
                for n in range(GROUPS):
                    if it.outs and n in (8, 30):
                        it.wait(dve, ln1_step if n == 8 else ln2_step, 2, -1, 1)
                    if it.scan:
                        scan(it, n)
                        if n % 4 == 3:
                            weigh(it, n // 4)
                    dense(it, n)
                if it.k0 == -1:
                    late_setup()

            run(dve, iteration)


_NAMES = ["x", "norm_w", "in_proj_w", "conv_w", "conv_b", "x_proj_w", "dt_proj_w", "dt_proj_b", "A_log", "D",
          "out_proj_w"]
_INS = ["L0_attn_" + n for n in _NAMES] + ["L0_ffn_w_gate", "L0_ffn_w_up", "L0_ffn_w_down"]


def kernel(**inputs):
    import numpy as np
    import concourse.bacc as bacc
    from concourse.bass_utils import run_bass_kernel_spmd

    nc = bacc.Bacc("TRN2", target_bir_lowering=False, num_devices=1)
    arrays, args = {}, []
    for name in _INS:
        a = np.ascontiguousarray(inputs[name])
        arrays[name + "_in"] = a
        args.append(nc.dram_tensor(name + "_in", a.shape, mybir.dt.from_np(a.dtype), kind="ExternalInput").ap())
    shape = np.shape(inputs["L0_attn_x"])
    out = nc.dram_tensor("out_dram", shape, mybir.dt.float32, kind="ExternalOutput").ap()
    mamba_swiglu_postln(nc, *args, out)
    r = run_bass_kernel_spmd(nc, [arrays], core_ids=[0])
    return r.results[0]["out_dram"]
```

```python
import concourse.bass as bass
from concourse import mybir
from contextlib import ExitStack


def mamba_swiglu_postln(nc, x, norm_w, in_w, conv_w, conv_b, xp_w, dt_w, dt_b, a_log, d_skip, out_w,
                        gate_w, up_w, down_w, out):
    f32, f32r, i32 = mybir.dt.float32, mybir.dt.float32r, mybir.dt.int32
    ALU, ACT, AX = mybir.AluOpType, mybir.ActivationFunctionType, mybir.AxisListType

    P = 128
    H = P // 2
    B, T, M = x.shape
    TILES = T // P
    DI = out_w.shape[1]
    HALVES = DI // P
    NS = a_log.shape[1]
    R = dt_w.shape[1]
    TAPS = conv_w.shape[2]
    J = P // NS
    GH = P // J
    QUADS = DI // J // 4
    QH = QUADS // HALVES
    GROUPS = 4 * QUADS
    HID = gate_w.shape[0] // P
    XB = R + NS
    WSCALE = 1.0 / 127.0
    SILU2 = WSCALE * WSCALE * WSCALE / 2
    EPS = 1e-5
    RING = 4
    DRIVES = 3

    ctx = ExitStack()
    with ctx:
        def sb(name, shape, dt=f32):
            return ctx.enter_context(nc.sbuf_tensor(name, shape, dt))

        def pair(name, shape, dt=f32):
            return [sb(f"{name}{i}", shape, dt) for i in range(2)]

        def pb(name):
            return ctx.enter_context(nc.psum_tensor(name, [P, T], f32))

        def sem(name):
            return ctx.enter_context(nc.semaphore(name))

        in_t = sb("in_t", [M, 2 * HALVES, P])
        xb_t = sb("xb_t", [P, HALVES, XB])
        xc_t = sb("xc_t", [P, HALVES, J, NS])
        dt_t = sb("dt_t", [R, HALVES, P])
        out_t = sb("out_t", [P, HALVES, M])
        gate_t = sb("gate_t", [M, HID, P], f32r)
        up_t = sb("up_t", [M, HID, P], f32r)
        down_t = sb("down_t", [P, HID, M])
        nw = sb("nw", [M, 1])
        cw = sb("cw", [P, HALVES, TAPS])
        cb = sb("cb", [P, HALVES])
        dtb = sb("dtb", [P, HALVES])
        dsk = sb("dsk", [P, HALVES])
        dhalf = sb("dhalf", [P, HALVES])
        a_exp = sb("a_exp", [P, DI // J])
        a_neg = sb("a_neg", [P, DI // J])
        ident = sb("ident", [P, P])
        perm = sb("perm", [P, P])
        spread = sb("spread", [P, GH // 2, P], f32r)
        lane_f = sb("lane_f", [P, J])
        gather = sb("gather", [P, QH, 4 * J])
        powm = sb("powm", [P, B * TILES])
        x_all = sb("x_all", [P, B * TILES, M])
        x_ss = sb("x_ss", [P, B * TILES])
        x_ms = sb("x_ms", [P, B * TILES])
        x_rs = sb("x_rs", [P, B * TILES])
        hx = sb("hx", [P, TILES, M])
        h_t = sb("h_t", [M, T])
        xs = sb("xs", [P, HALVES, TAPS - 1 + T])
        tap = [sb(f"tap{i}", [P, HALVES, T]) for i in range(TAPS)]
        conv = sb("conv", [P, HALVES, T])
        conv_th = sb("conv_th", [P, HALVES, T])
        res_th = sb("res_th", [P, HALVES, T])
        z_abs, z_pos, z_ln, z_w, z_e, z_c, du = tap[1], tap[3], tap[0], tap[2], conv_th, res_th, tap[1]
        xd = sb("xd", [XB, T])
        delta = sb("delta", [P, HALVES, T])
        d_hi = sb("d_hi", [P, HALVES, T], f32r)
        d_lo = sb("d_lo", [P, HALVES, T], f32r)
        u2 = pair("u2_", [P, HALVES, T])
        sres = pair("sres", [P, HALVES, T])
        du_t = pair("du_t", [P, QUADS, TILES, 4 * J])
        b_t = pair("b_t", [P, TILES, NS])
        c_rep = pair("c_rep", [P, T])
        d_pack = pair("d_pack", [P, 2 * HALVES, T], f32r)
        y_out_all = sb("y_out", [P, 2, TILES * M])
        y_out = [y_out_all[:, i, :].rearrange("p (i m) -> p i m", m=M) for i in range(2)]
        prod_all = sb("prod", [P, 2, TILES * 4 * P])
        prod = [prod_all[:, i, :].rearrange("p (i c f) -> p i c f", i=TILES, c=4) for i in range(2)]
        decay = [sb(f"decay{i}", [P, T]) for i in range(RING)]
        state = sb("state", [P, 4, T])
        weighted = pair("weighted", [P, 4, T])
        x_sq = prod_all[:, :, :].rearrange("p a f -> p (a f)")

        def room(buf):
            flat, at = buf[:, :, :].rearrange("p c t -> p (c t)"), [0]

            def cut(rows, cols, dt=f32):
                at[0] += cols
                assert at[0] <= 4 * T
                return flat[0:rows, at[0] - cols:at[0]].bitcast(dt)
            return cut

        cut = room(state)
        in_raw = cut(P, 2 * HALVES * M).rearrange("p (c m) -> p c m", m=M)
        xp_raw, dt_raw = cut(XB + NS, DI), cut(P, HALVES * R).rearrange("p (h r) -> p h r", r=R)
        al_raw, out_raw = cut(DI // J, P), cut(M, DI)
        cut = room(weighted[0])
        gate_raw, up_raw = [cut(P, HID * M, i32).rearrange("p (b m) -> p b m", m=M) for _ in range(2)]
        down_raw = cut(M, HID * P, i32)
        cut = room(weighted[1])
        gate_f, up_f = [cut(P, HID * M).rearrange("p (b m) -> p b m", m=M) for _ in range(2)]
        down_f = cut(M, HID * P)
        spread_f = y_out_all[:, :, :].rearrange("p a f -> p (a f)").rearrange(
            "p (s j n) -> p s j n", j=J, n=NS)
        g = sb("g", [P, HALVES, T])
        r1 = sb("r1", [P, TILES, M])
        st1 = sb("st1", [P, TILES, 6])
        mv1 = sb("mv1", [P, TILES, 2])
        ve1 = sb("ve1", [P, TILES])
        rs1 = sb("rs1", [P, TILES])
        x1 = sb("x1", [P, TILES, M])
        x1_hi = sb("x1_hi", [M, T], f32r)
        x1_lo = sb("x1_lo", [M, T], f32r)
        g_th = sb("g_th", [P, 2, T])
        g_act = sb("g_act", [P, HID, T])
        r2 = sb("r2", [P, TILES, M])
        st2 = sb("st2", [P, TILES, 6])
        mv2 = sb("mv2", [P, TILES, 2])
        ve2 = sb("ve2", [P, TILES])
        rs2 = sb("rs2", [P, TILES])

        delta_ps = pb("delta_ps")
        drive_ps = [pb(f"drive_ps{i}") for i in range(DRIVES)]
        y_ps = pb("y_ps")
        dense_ps = [pb(f"dense_ps{i}") for i in range(3)]

        ld_x0 = sem("ld_x0")
        ld_x = sem("ld_x")
        ld_in = sem("ld_in")
        ld_xp = sem("ld_xp")
        ld_vec = sem("ld_vec")
        ld_out = sem("ld_out")
        ld_ffn = sem("ld_ffn")
        consts0 = sem("consts0")
        consts = sem("consts")
        consts_dve = sem("consts_dve")
        spread_ready = sem("spread_ready")
        wt_turned = sem("wt_turned")
        wt_taken = sem("wt_taken")
        ffn_float = sem("ffn_float")
        a_exped = sem("a_exped")
        a_ready = sem("a_ready")
        sq_ready = sem("sq_ready")
        ms_step = sem("ms_step")
        ms_ready = sem("ms_ready")
        rs_ready = sem("rs_ready")
        hx_ready = sem("hx_ready")
        full = [sem(f"full{i}") for i in range(3)]
        taken = [sem(f"taken{i}") for i in range(3)]
        taps_ready = sem("taps_ready")
        conv_part = sem("conv_part")
        conv_ready = sem("conv_ready")
        conv_th_ready = sem("conv_th_ready")
        res_th_ready = sem("res_th_ready")
        u2_ready = sem("u2_ready")
        z_step = sem("z_step")
        z_ln_ready = sem("z_ln_ready")
        soft_step = sem("soft_step")
        delta_ready = sem("delta_ready")
        du_ready = sem("du_ready")
        hi_ready = sem("hi_ready")
        lo_ready = sem("lo_ready")
        packed = sem("packed")
        delta_spread = sem("delta_spread")
        decay_ready = sem("decay_ready")
        prod_ready = sem("prod_ready")
        drive_ready = sem("drive_ready")
        scanned = sem("scanned")
        weighted_ready = sem("weighted_ready")
        summed = sem("summed")
        y_taken = sem("y_taken")
        g_ready = sem("g_ready")
        r1_ready = sem("r1_ready")
        ln1_step = sem("ln1_step")
        ve1_ready = sem("ve1_ready")
        rs1_ready = sem("rs1_ready")
        x1_ready = sem("x1_ready")
        x1_hi_ready = sem("x1_hi_ready")
        g_th_ready = sem("g_th_ready")
        g_act_ready = sem("g_act_ready")
        r2_ready = sem("r2_ready")
        ln2_step = sem("ln2_step")
        ve2_ready = sem("ve2_ready")
        rs2_ready = sem("rs2_ready")
        y_ready = sem("y_ready")
        y_free = [sem(f"y_free{i}") for i in range(2)]

        IN_JOBS = [(2, 0, "h"), (3, 1, "xs0"), (4, 2, "xs1"), (8, 1, "res0"), (9, 2, "res1"), (18, 0, "xd"),
                   (20, 0, "z0"), (21, 1, "z1"), (22, 2, "bt"), (27, 1, "dut0"), (28, 2, "dut1"),
                   (30, 2, "crep")]
        OUT_JOBS = [(5, 0, "proj"), (13, 0, "x1"), (16, 1, "gate0"), (17, 2, "up0"), (22, 0, "gate1"),
                    (23, 1, "up1"), (24, 2, "gate2"), (26, 0, "up2"), (29, 0, "down0"), (29, 1, "down1")]
        ALL_JOBS = sorted(IN_JOBS + OUT_JOBS, key=lambda job: job[0])
        BANK = {name: bank for _, bank, name in ALL_JOBS}

        def jobs_of(k):
            return [n for _, _, n in (IN_JOBS if k < 1 else OUT_JOBS if k > B - 2 else ALL_JOBS)]

        class Iteration:

            def __init__(self, k0, ahead=0):
                self.k0, self.ahead = k0, ahead
                self.scan = 0 <= k0 < B
                self.ins = k0 < B - 1
                self.outs = k0 > 0
                self.now, self.next = k0 % 2, (k0 + 1) % 2
                self.names = jobs_of(k0)
                earlier = [n for k in range(-1, k0) for n in jobs_of(k)]
                self.before = [sum(BANK[n] == b for n in earlier) for b in range(3)]

            def count(self, each, batch, n):
                return each * (self.k0 + batch) + n + each * self.ahead

            def wait(self, eng, s, each, batch, n):
                if each * (self.k0 + batch) + n > 0:
                    eng.wait_ge(s, self.count(each, batch, n))

            def job_count(self, name, less=0):
                mine = [n for n in self.names if BANK[n] == BANK[name]]
                at = self.before[BANK[name]] + mine.index(name) + 1 - less
                return at, at + sum(b == BANK[name] for b in BANK.values()) * self.ahead

            def wait_full(self, eng, name):
                eng.wait_ge(full[BANK[name]], self.job_count(name)[1])

            def wait_taken(self, eng, name):
                eng.wait_ge(taken[BANK[name]], self.job_count(name)[1])

            def wait_free(self, eng, name):
                at, value = self.job_count(name, 1)
                if at > 0:
                    eng.wait_ge(taken[BANK[name]], value)

            def ps(self, name):
                return dense_ps[BANK[name]]

            def take(self, ins, name):
                ins.then_inc(taken[BANK[name]], 1)

        def run(eng, iteration):
            for k in (-1, 0):
                iteration(Iteration(k))
            with eng.Fori(0, (B - 2) // 2) as i:
                for k in (1, 2):
                    iteration(Iteration(k, 2 * i))
            for k in (B - 1, B):
                iteration(Iteration(k))

        block = ctx.enter_context(nc.Block())

        @block.sync
        def _(sp):
            for s in y_free:
                sp.sem_inc(s, 16)
            xv = x.rearrange("b (i t) m -> t (b i) m", t=P)
            sp.dma_start(x_all[:, 0:TILES, :], xv[:, 0:TILES, :]).then_inc(ld_x0, 16)
            sp.dma_start(xp_raw[:, :], xp_w).then_inc(ld_xp, 16)
            sp.dma_start(dt_raw[:, :, :], dt_w.rearrange("(h d) r -> d h r", h=HALVES)).then_inc(ld_xp, 16)
            sp.dma_start(x_all[:, TILES:, :], xv[:, TILES:, :]).then_inc(ld_x, 16)
            sp.dma_start(gate_raw[:, :, :], gate_w.rearrange("(b h) m -> h b m", h=P)).then_inc(ld_ffn, 16)
            sp.dma_start(up_raw[:, :, :], up_w.rearrange("(b h) m -> h b m", h=P)).then_inc(ld_ffn, 16)
            sp.dma_start(down_raw[:, :], down_w).then_inc(ld_ffn, 16)

            y_rows = out.rearrange("b t m -> (b t) m")

            def iteration(it):
                def value(v):
                    return v if isinstance(v, int) else sp.snap(v)

                both, done, row = value(it.count(1, 1, 1)), value(it.count(1, -1, 1)), value((it.k0 - 1 + it.ahead) * T)
                if it.ins:
                    sp.wait_ge(hi_ready, both)
                    sp.wait_ge(lo_ready, both)
                    for part, src in enumerate((d_hi, d_lo)):
                        for h in range(HALVES):
                            for half in range(2):
                                sp.dma_start(d_pack[it.next][H * part:H * part + H, 2 * h + half, :].bitcast(f32),
                                             src[H * half:H * half + H, h, :].bitcast(f32)).then_inc(packed, 16)
                if it.outs:
                    rows = y_rows[row:row + T, :] if isinstance(row, int) else y_rows[bass.ds(row, T), :]
                    sp.wait_ge(y_ready, done)
                    sp.dma_start(rows.rearrange("(i t) m -> t i m", t=P), y_out[it.next][:, :, :]
                                 ).then_inc(y_free[it.next], 16)

            run(sp, iteration)
            for s in y_free:
                sp.wait_ge(s, 16 + 16 * (B // 2))

        @block.tensor
        def _(pe):
            mm, turn = pe.matmul, pe.transpose
            pe.wait_ge(consts, 1)
            pe.wait_ge(ld_in, 16)
            for c in range(2 * HALVES):
                last = turn(delta_ps[:, c * P:(c + 1) * P], in_raw[:, c, :], ident[:, :])
            last.then_inc(wt_turned, 1)
            pe.wait_ge(ld_xp, 32)
            for h in range(HALVES):
                turn(dense_ps[0][:, h * P:h * P + XB + NS], xp_raw[:, h * P:(h + 1) * P],
                     ident[0:XB + NS, 0:XB + NS])
                last = turn(dense_ps[0][0:R, (2 + h) * P:(3 + h) * P], dt_raw[:, h, :], ident[:, :])
            last.then_inc(wt_turned, 1)
            pe.wait_ge(ld_out, 32)
            turn(drive_ps[0][:, 0:DI // J], al_raw[:, :], ident[0:DI // J, 0:DI // J])
            for h in range(HALVES):
                last = turn(drive_ps[0][:, (1 + h) * P:(2 + h) * P], out_raw[:, h * P:(h + 1) * P], ident[:, :])
            last.then_inc(wt_turned, 1)

            def ffn_weights():
                pe.wait_ge(ffn_float, 3)
                for ps, w in ((drive_ps[1], lambda b: gate_f[:, b, :]), (dense_ps[1], lambda b: up_f[:, b, :]),
                              (dense_ps[2], lambda b: down_f[:, b * P:(b + 1) * P])):
                    for b in range(HID):
                        last = turn(ps[:, b * P:(b + 1) * P], w(b), ident[:, :])
                    last.then_inc(wt_turned, 1)

            def spread_delta(it, n, batch=0):
                side = it.now if batch == 0 else it.next
                h, q, c = n // 4 // QH, n // 4 % QH, n % 4
                gl = 4 * c + q
                if n == 0:
                    it.wait(pe, packed, 16 * 4 * HALVES, batch, 16 * 4 * HALVES)
                it.wait(pe, decay_ready, GROUPS, batch, n)
                mm(delta_ps[:, :], spread[:, gl % J, :], d_pack[side][:, 2 * h + gl // J, :],
                   start=True, stop=True).then_inc(delta_spread, 1)

            def turn_drive(it, n):
                quad, c = n // 4, n % 4
                if c == 0:
                    it.wait(pe, prod_ready, QUADS, 0, quad + 1)
                last = n - DRIVES if n >= DRIVES else (GROUPS - 1 - n) // DRIVES * DRIVES + n - GROUPS
                it.wait(pe, scanned, GROUPS, 0, last + 1)
                for i in range(TILES):
                    last = turn(drive_ps[n % DRIVES][:, i * P:(i + 1) * P], prod[quad % 2][:, i, c, :], ident[:, :])
                last.then_inc(drive_ready, 1)

            def sum_states(it, quad, batch=0):
                h, q = quad // QH, quad % QH
                it.wait(pe, weighted_ready, QUADS, batch, quad + 1)
                if q == 0:
                    it.wait(pe, y_taken, HALVES, batch, h)
                for c in range(4):
                    last = mm(y_ps[32 * c:32 * c + 32, :], gather[:, q, :], weighted[quad % 2][:, c, :],
                              start=(q == 0), stop=(q == QH - 1), tile_position=(0, 32 * c))
                last.then_inc(summed, 1)

            def job(it, name):
                ps, kind, n = it.ps(name), name, 0
                if name != "x1" and name[-1].isdigit():
                    kind, n = name[:-1], int(name[-1])
                it.wait_free(pe, name)
                if kind == "h":
                    it.wait(pe, hx_ready, 1, 1, 1)
                    for i in range(TILES):
                        last = turn(ps[:, i * P:(i + 1) * P], hx[:, i, :], ident[:, :])
                elif kind in ("xs", "res"):
                    if kind == "xs" and n == 0:
                        it.wait_taken(pe, "h")
                    last = mm(ps[:, :], in_t[:, n + (HALVES if kind == "res" else 0), :], h_t[:, :],
                              start=True, stop=True)
                elif kind in ("xd", "crep"):
                    it.wait(pe, u2_ready, 1, 1, 1)
                    for h in range(HALVES):
                        w = xb_t[:, h, :] if kind == "xd" else xc_t[:, h, :, :].rearrange("p j n -> p (j n)")
                        last = mm(ps[0:XB if kind == "xd" else P, :], w, u2[it.next][:, h, :],
                                  start=(h == 0), stop=(h == HALVES - 1))
                elif kind == "z":
                    it.wait_taken(pe, "xd")
                    last = mm(ps[:, :], dt_t[:, n, :], xd[0:R, :], start=True, stop=True)
                elif kind == "bt":
                    for i in range(TILES):
                        last = turn(ps[:, i * XB:(i + 1) * XB], xd[:, i * P:(i + 1) * P], ident[0:XB, 0:XB])
                elif kind == "dut":
                    it.wait(pe, du_ready, 1, 1, 1)
                    for i in range(2):
                        for h in range(HALVES):
                            last = turn(ps[:, (i * HALVES + h) * P:(i * HALVES + h + 1) * P],
                                        du[:, h, (2 * n + i) * P:(2 * n + i + 1) * P], perm[:, :])
                elif kind == "proj":
                    it.wait(pe, g_ready, HALVES, -1, HALVES)
                    for i in range(TILES):
                        for h in range(HALVES):
                            last = mm(ps[:, i * P:(i + 1) * P], g[:, h, i * P:(i + 1) * P],
                                      out_t[:, h, :], start=(h == 0), stop=(h == HALVES - 1))
                elif kind == "x1":
                    it.wait(pe, x1_ready, 1, -1, 1)
                    for i in range(TILES):
                        last = turn(ps[:, i * P:(i + 1) * P], x1[:, i, :], ident[:, :])
                elif kind in ("gate", "up"):
                    if name == "gate0":
                        it.wait(pe, x1_hi_ready, 1, -1, 1)
                        it.wait_taken(pe, "x1")
                    w = (gate_t if kind == "gate" else up_t)[:, n, :]
                    mm(ps[:, :], w, x1_hi[:, :], start=True, stop=False)
                    last = mm(ps[:, :], w, x1_lo[:, :], start=False, stop=True)
                elif kind == "down":
                    it.wait_taken(pe, f"up{HID - 1}")
                    for i in range(2):
                        for b in range(HID):
                            last = mm(ps[:, i * P:(i + 1) * P], g_act[:, b, (2 * n + i) * P:(2 * n + i + 1) * P],
                                      down_t[:, b, :], start=(b == 0), stop=(b == HID - 1))
                last.then_inc(full[BANK[name]], 1)

            def iteration(it):
                todo = list(it.names)
                when = {name: step for step, _, name in ALL_JOBS}
                if it.k0 == -1:
                    pe.wait_ge(wt_taken, 3)
                for n in range(GROUPS):
                    if it.scan:
                        if n + 1 < GROUPS:
                            spread_delta(it, n + 1)
                        turn_drive(it, n)
                        if n % 4 == 2 and (n > 2 or it.k0 > 0):
                            if n > 2:
                                sum_states(it, n // 4 - 1)
                            else:
                                sum_states(it, QUADS - 1, -1)
                    elif n == 2 and it.k0 == B:
                        sum_states(it, QUADS - 1, -1)
                    while todo and when[todo[0]] <= n:
                        job(it, todo.pop(0))
                if it.ins:
                    if it.k0 == -1:
                        ffn_weights()
                        pe.wait_ge(wt_taken, 6)
                        pe.wait_ge(spread_ready, 1)
                    spread_delta(it, 0, 1)

            run(pe, iteration)

        @block.scalar
        def _(act):
            A = act.activation
            act.dma_start(in_raw[:, :, :], in_w.rearrange("(c d) m -> d c m", d=P)).then_inc(ld_in, 16)
            act.dma_start(nw[:, :], norm_w.rearrange("(m o) -> m o", o=1)).then_inc(ld_vec, 16)
            act.dma_start(cw[:, :, :], conv_w.rearrange("(h d) o j -> d h (o j)", h=HALVES)).then_inc(ld_vec, 16)
            with nc.allow_non_contiguous_dma(reason="a few vectors, once"):
                for dst, src in ((cb, conv_b), (dtb, dt_b), (dsk, d_skip)):
                    act.dma_start(dst[:, :], src.rearrange("(h d) -> d h", h=HALVES)).then_inc(ld_vec, 16)
            act.dma_start(al_raw[:, :], a_log.rearrange("(g j) n -> g (j n)", j=J)).then_inc(ld_out, 16)
            act.dma_start(out_raw[:, :], out_w).then_inc(ld_out, 16)
            act.wait_ge(ld_x0, 16)
            flat = x_all[:, :, :].rearrange("p b m -> p (b m)")
            first = TILES * M
            A(x_sq[:, 0:first], flat[:, 0:first], ACT.Square).then_inc(sq_ready, 1)
            act.wait_ge(ld_vec, 16 * 5)

            def late_setup():
                act.wait_ge(wt_turned, 3)
                A(a_exp[:, :], drive_ps[0][:, 0:DI // J], ACT.Exp).then_inc(a_exped, 1)
                act.wait_ge(consts, 1)
                A(spread[:, :, :], spread_f[:, :, :, :].rearrange("p s j n -> p s (j n)"), ACT.Copy
                  ).then_inc(spread_ready, 1)
                act.wait_ge(ld_x, 16)
                A(x_sq[:, first:], flat[:, first:], ACT.Square).then_inc(sq_ready, 1)
                act.wait_ge(a_ready, 1)

            def exp_decay(it, n):
                h, q, c = n // 4 // QH, n // 4 % QH, n % 4
                it.wait(act, delta_spread, GROUPS, 0, n + 1)
                it.wait(act, scanned, GROUPS, 0, n + 1 - RING)
                col = GH * h + 4 * c + q
                A(decay[n % RING][:, :], delta_ps[:, :], ACT.Exp, scale=a_neg[:, col:col + 1]
                  ).then_inc(decay_ready, 1)

            def dense(it, step):
                if it.ins:
                    if step == 2:
                        it.wait_full(act, "h")
                        it.take(A(h_t[:, :], it.ps("h")[:, :], ACT.Copy, scale=nw[:, 0:1]), "h")
                    if step in (4, 5):
                        name = f"xs{step - 4}"
                        it.wait_full(act, name)
                        if step == 4:
                            it.wait(act, conv_ready, 1, 0, 1)
                        it.take(A(xs[:, step - 4, TAPS - 1:], it.ps(name)[:, :], ACT.Copy), name)
                    if 5 <= step < 9:
                        h = (step - 5) // 2
                        if step % 2:
                            it.wait_taken(act, f"xs{h}")
                            if step == 5 and it.k0 == -1:
                                act.wait_ge(consts_dve, 1)
                        for j in range(2 * (1 - step % 2), 2 * (1 - step % 2) + 2):
                            A(tap[j][:, h, :], xs[:, h, j:j + T], ACT.Identity, scale=cw[:, h, j:j + 1],
                              bias=cb[:, h:h + 1] if j == 0 else 0.0).then_inc(taps_ready, 1)
                    if step in (9, 10):
                        name = f"res{step - 9}"
                        it.wait_full(act, name)
                        A(res_th[:, step - 9, :], it.ps(name)[:, :], ACT.Tanh, scale=0.5).then_inc(res_th_ready, 1)
                    if step == 15:
                        it.wait(act, conv_ready, 1, 1, 1)
                        A(conv_th[:, :, :], conv[:, :, :], ACT.Tanh, scale=0.5).then_inc(conv_th_ready, 1)
                    if step == 19:
                        it.wait_full(act, "xd")
                        it.take(A(xd[:, :], it.ps("xd")[0:XB, :], ACT.Copy), "xd")
                    if step == 31:
                        it.wait_full(act, "crep")
                        it.take(A(c_rep[it.next][:, :], it.ps("crep")[:, :], ACT.Copy), "crep")
                    if step in (21, 22):
                        h, name = step - 21, f"z{step - 21}"
                        it.wait_full(act, name)
                        A(z_abs[:, h, :], it.ps(name)[:, :], ACT.Abs, bias=dtb[:, h:h + 1]).then_inc(z_step, 1)
                        it.take(A(z_pos[:, h, :], it.ps(name)[:, :], ACT.Relu, bias=dtb[:, h:h + 1]), name)
                    if step == 22:
                        it.wait(act, z_step, 3, 1, 2)
                        A(z_e[:, :, :], z_abs[:, :, :], ACT.Exp, scale=-1.0).then_inc(z_step, 1)
                        it.wait(act, z_step, 3, 1, 3)
                        A(z_ln[:, :, :], z_e[:, :, :], ACT.Ln, bias=1.0).then_inc(z_ln_ready, 1)
                    if step == 23:
                        it.wait_full(act, "bt")
                        it.take(A(b_t[it.next][:, :, :],
                                  it.ps("bt")[:, 0:TILES * XB].rearrange("p (i r) -> p i r", i=TILES)[:, :, R:XB],
                                  ACT.Copy), "bt")
                    if step == 26:
                        it.wait(act, delta_ready, 1, 1, 1)
                        A(d_hi[:, :, :], delta[:, :, :], ACT.Copy).then_inc(hi_ready, 1)
                    if step in (28, 29):
                        n, name = step - 28, f"dut{step - 28}"
                        it.wait_full(act, name)
                        dst = du_t[it.next][:, :, 2 * n:2 * n + 2, :]
                        src = it.ps(name)[:, :].rearrange("p (i e f) -> p e i f", i=2, f=4 * J)
                        it.take(A(dst, src, ACT.Copy), name)
                if it.outs:
                    if step == 14:
                        it.wait_full(act, "x1")
                        A(x1_hi[:, :], it.ps("x1")[:, :], ACT.Copy).then_inc(x1_hi_ready, 1)
                    for b, at in enumerate((17, 23, 25)):
                        if step == at:
                            it.wait_full(act, f"gate{b}")
                            A(g_th[:, b % 2, :], it.ps(f"gate{b}")[:, :], ACT.Tanh, scale=WSCALE / 2
                              ).then_inc(g_th_ready, 1)

            def iteration(it):
                if it.scan:
                    exp_decay(it, 0)
                for n in range(GROUPS):
                    if it.scan and n + 1 < GROUPS:
                        exp_decay(it, n + 1)
                    dense(it, n)
                if it.k0 == -1:
                    late_setup()

            run(act, iteration)

        @block.gpsimd
        def _(pool):
            TT = pool.tensor_tensor
            for t in (ident, perm, spread_f):
                pool.memset(t[:], 0.0).then_inc(consts0, 1)
            pool.memset(lane_f[:, :], 1.0).then_inc(consts0, 1)
            pool.memset(powm[:, :], -0.5).then_inc(consts0, 1)
            pool.wait_ge(consts0, 5)
            sel = pool.affine_select
            sel(out=ident[:, :], in_=ident[:, :], compare_op=ALU.not_equal, fill=1.0, base=0,
                pattern=[[-1, P]], channel_multiplier=1)
            sel(out=perm[:, :], in_=perm[:, :], compare_op=ALU.not_equal, fill=1.0, base=0,
                pattern=[[-J, 4], [-4 * J, 4], [-1, J]], channel_multiplier=1)
            sel(out=lane_f[:, :], in_=lane_f[:, :], compare_op=ALU.is_ge, fill=0.0, base=0,
                pattern=[[-NS, J]], channel_multiplier=1).then_inc(consts0, 1)
            pool.wait_ge(consts0, 6)
            sel(out=lane_f[:, :], in_=lane_f[:, :], compare_op=ALU.is_ge, fill=0.0, base=NS - 1,
                pattern=[[NS, J]], channel_multiplier=-1)
            sel(out=spread_f[:], in_=spread_f[:], compare_op=ALU.not_equal, fill=1.0, base=0,
                pattern=[[-J, GH // 2], [-1, J], [0, NS]], channel_multiplier=1).then_inc(consts0, 1)
            pool.wait_ge(consts0, 7)
            sel(out=spread_f[:], in_=spread_f[:], compare_op=ALU.not_equal, fill=1.0, base=-H,
                pattern=[[-J, GH // 2], [-1, J], [0, NS]], channel_multiplier=1).then_inc(consts, 1)
            pool.wait_ge(ms_ready, 1)
            TT(x_rs[:, 0:TILES], x_ms[:, 0:TILES], powm[:, 0:TILES], ALU.pow).then_inc(rs_ready, 1)
            pool.wait_ge(rs_ready, 1)

            def scale_x(it):
                it.wait(pool, u2_ready, 1, 0, 1)
                lo = (it.k0 + 1 + it.ahead) * TILES
                xk = x_all[:, bass.ds(lo, TILES), :] if not isinstance(lo, int) else x_all[:, lo:lo + TILES, :]
                rk = x_rs[:, bass.ds(lo, TILES)] if not isinstance(lo, int) else x_rs[:, lo:lo + TILES]
                TT(hx[:, :, :], xk, rk.unsqueeze(2).broadcast_to([P, TILES, M]), ALU.mult).then_inc(hx_ready, 1)

            def multiply(it, quad):
                if quad == 0:
                    pool_wait_in(it)
                it.wait(pool, drive_ready, GROUPS, 0, 4 * (quad - 1))
                a = du_t[it.now][:, quad, :, :].unsqueeze(3).broadcast_to([P, TILES, 4 * J, NS])
                b = b_t[it.now][:, :, :].unsqueeze(2).broadcast_to([P, TILES, 4 * J, NS])
                o = prod[quad % 2][:, :, :, :].rearrange("p i c (j n) -> p i (c j) n", n=NS)
                TT(o, a, b, ALU.mult).then_inc(prod_ready, 1)

            def pool_wait_in(it):
                prev = Iteration(it.k0 - 1, it.ahead)
                for name in ("dut0", "dut1"):
                    prev.wait_taken(pool, name)

            def first_quad(it):
                multiply(Iteration(it.k0 + 1, it.ahead), 0)

            def iteration(it):
                if it.ins:
                    scale_x(it)
                for quad in range(1, QUADS):
                    if it.scan:
                        multiply(it, quad)
                    if it.outs and quad == 3:
                        it.wait(pool, ve1_ready, 1, -1, 1)
                        TT(rs1[:, :], ve1[:, :], powm[:, 0:TILES], ALU.pow).then_inc(rs1_ready, 1)
                    if it.ins and quad == 3:
                        it.wait(pool, taps_ready, HALVES * TAPS, 1, HALVES * TAPS)
                        it.wait(pool, u2_ready, 1, 0, 1)
                        TT(tap[0][:], tap[0][:], tap[1][:], ALU.add).then_inc(conv_part, 1)
                        TT(tap[2][:], tap[2][:], tap[3][:], ALU.add).then_inc(conv_part, 1)
                        it.wait(pool, conv_part, 2, 1, 2)
                        TT(conv[:], tap[0][:], tap[2][:], ALU.add).then_inc(conv_ready, 1)
                if it.ins:
                    it.wait(pool, hi_ready, 1, 1, 1)
                    it.wait(pool, packed, 16 * 4 * HALVES, 0, 16 * 4 * HALVES)
                    TT(d_lo[:], delta[:], d_hi[:].bitcast(f32), ALU.subtract).then_inc(lo_ready, 1)
                if it.k0 == -1:
                    pool.wait_ge(ms_ready, 2)
                if it.ins:
                    first_quad(it)
                if it.outs:
                    it.wait(pool, ve2_ready, 1, -1, 1)
                    TT(rs2[:, :], ve2[:, :], powm[:, 0:TILES], ALU.pow).then_inc(rs2_ready, 1)
                if it.k0 == -1:
                    pool.wait_ge(ld_ffn, 48)
                    pool.tensor_copy(gate_f[:], gate_raw[:]).then_inc(ffn_float, 1)
                    pool.tensor_copy(up_f[:], up_raw[:]).then_inc(ffn_float, 1)
                    pool.tensor_copy(down_f[:], down_raw[:]).then_inc(ffn_float, 1)
                    pool.wait_ge(ms_ready, 2)
                    TT(x_rs[:, TILES:], x_ms[:, TILES:], powm[:, TILES:], ALU.pow).then_inc(rs_ready, 1)
                    pool.wait_ge(rs_ready, 2)

            run(pool, iteration)

        @block.vector
        def _(dve):
            TT, TS, STT = dve.tensor_tensor, dve.tensor_scalar, dve.scalar_tensor_tensor

            def mean_square(n, lo, hi):
                dve.wait_ge(sq_ready, n)
                dve.tensor_reduce(out=x_ss[:, lo:hi], in_=x_sq[:, lo * M:hi * M].rearrange("p (t m) -> p t m", m=M),
                                  op=ALU.add, axis=AX.X).then_inc(ms_step, 1)
                dve.wait_ge(ms_step, n)
                TS(x_ms[:, lo:hi], x_ss[:, lo:hi], 1.0 / M, EPS, ALU.mult, ALU.add).then_inc(ms_ready, 1)

            dve.memset(xs[:, :, 0:TAPS - 1], 0.0).then_inc(consts_dve, 1)
            dve.memset(gather[:, :, :], 0.0).then_inc(consts_dve, 1)
            mean_square(1, 0, TILES)
            dve.wait_ge(wt_turned, 1)
            dve.tensor_copy(in_t[:, :, :].rearrange("p c d -> p (c d)"), delta_ps[:, :]).then_inc(wt_taken, 1)
            dve.wait_ge(wt_turned, 2)
            wx = dense_ps[0][:, 0:HALVES * P].rearrange("p (h r) -> p h r", h=HALVES)
            TS(xb_t[:, :, 0:R], wx[:, :, 0:R], 0.5, None, ALU.mult)
            TS(xb_t[:, :, R:XB], wx[:, :, R:XB], 0.25, None, ALU.mult)
            for h in range(HALVES):
                TS(xc_t[:, h, :, :], wx[:, h, XB:XB + NS].unsqueeze(1).broadcast_to([P, J, NS]), 0.5, None, ALU.mult)
            dve.tensor_copy(dt_t[:, :, :], dense_ps[0][0:R, HALVES * P:2 * HALVES * P].rearrange(
                "p (h d) -> p h d", h=HALVES)).then_inc(wt_taken, 1)
            dve.wait_ge(wt_turned, 3)
            TS(out_t[:, :, :], drive_ps[0][:, P:(1 + HALVES) * P].rearrange("p (h m) -> p h m", h=HALVES),
               0.5, None, ALU.mult).then_inc(wt_taken, 1)
            dve.wait_ge(ld_vec, 16 * 5)
            TS(dhalf[:, :], dsk[:, :], 0.5, None, ALU.mult)
            dve.wait_ge(consts, 1)
            dve.wait_ge(consts_dve, 2)
            for q in range(QH):
                dve.tensor_copy(gather[:, q, q * J:(q + 1) * J], lane_f[:, :]).then_inc(consts_dve, 1)

            def late_setup():
                dve.wait_ge(a_exped, 1)
                TS(a_neg[:, :], a_exp[:, :], -1.0, None, ALU.mult).then_inc(a_ready, 1)
                mean_square(2, TILES, B * TILES)
                for n, (dst, ps) in enumerate(((gate_t, drive_ps[1]), (up_t, dense_ps[1]), (down_t, dense_ps[2]))):
                    dve.wait_ge(wt_turned, 4 + n)
                    dve.tensor_copy(dst[:, :, :].rearrange("p b h -> p (b h)"), ps[:, 0:HID * P]
                                    ).then_inc(wt_taken, 1)

            def scan(it, n):
                it.wait(dve, weighted_ready, QUADS, 0, n // 4)
                it.wait(dve, decay_ready, GROUPS, 0, n + 1)
                it.wait(dve, drive_ready, GROUPS, 0, n + 1)
                dve.tensor_tensor_scan(state[:, n % 4, :], decay[n % RING][:, :], drive_ps[n % DRIVES][:, :], 0.0,
                                       ALU.mult, ALU.add).then_inc(scanned, 1)

            def weigh(it, quad):
                it.wait(dve, scanned, GROUPS, 0, 4 * quad + 4)
                it.wait(dve, summed, QUADS, 0, quad - 1)
                if quad == 0:
                    prev = Iteration(it.k0 - 1, it.ahead)
                    prev.wait_taken(dve, "crep")
                TT(weighted[quad % 2][:, :, :], state[:, :, :],
                   c_rep[it.now][:, :].unsqueeze(1).broadcast_to([P, 4, T]), ALU.mult).then_inc(weighted_ready, 1)

            def combine(it, h, batch):
                side = it.now if batch == 0 else it.next
                it.wait(dve, summed, QUADS, batch, QH * (h + 1))
                STT(out=g[:, h, :], in0=u2[side][:, h, :], scalar=dhalf[:, h:h + 1], in1=y_ps[:, :],
                    op0=ALU.mult, op1=ALU.add).then_inc(y_taken, 1)
                it.wait(dve, y_taken, HALVES, batch, h + 1)
                TT(g[:, h, :], g[:, h, :], sres[side][:, h, :], ALU.mult).then_inc(g_ready, 1)

            def normalise(it, dst, r, mv, rs, rs_ready_, ready):
                it.wait(dve, rs_ready_, 1, -1, 1)
                for i in range(TILES):
                    last = TS(dst[:, i, :], r[:, i, :], mv[:, i, 0:1], rs[:, i:i + 1], ALU.subtract, ALU.mult)
                last.then_inc(ready, 1)

            def dense(it, step):
                if it.outs:
                    if step == 3:
                        combine(it, 1, -1)
                    if step == 6:
                        it.wait_full(dve, "proj")
                        lo = (it.k0 - 1 + it.ahead) * TILES
                        xk = x_all[:, lo:lo + TILES, :] if isinstance(lo, int) else x_all[:, bass.ds(lo, TILES), :]
                        it.take(STT(out=r1[:, :, :], in0=xk, scalar=2.0,
                                    in1=it.ps("proj")[:, :].rearrange("p (i m) -> p i m", m=M),
                                    op0=ALU.mult, op1=ALU.add), "proj")
                        it.wait_taken(dve, "proj")
                        for i in range(TILES):
                            last = dve.bn_stats(st1[:, i, :], r1[:, i, :])
                        last.then_inc(ln1_step, 1)
                    if step == 7:
                        for i in range(TILES):
                            last = dve.bn_aggr(mv1[:, i, :], st1[:, i, :])
                        last.then_inc(ln1_step, 1)
                        it.wait(dve, ln1_step, 2, -1, 2)
                        TS(ve1[:, :], mv1[:, :, 1], EPS, None, ALU.add).then_inc(ve1_ready, 1)
                    if step == 11:
                        normalise(it, x1, r1, mv1, rs1, rs1_ready, x1_ready)
                if it.ins:
                    if step in (10, 11):
                        h, name = step - 10, f"res{step - 10}"
                        it.wait(dve, res_th_ready, 2, 1, h + 1)
                        it.take(STT(out=sres[it.next][:, h, :], in0=res_th[:, h, :], scalar=1.0,
                                    in1=it.ps(name)[:, :], op0=ALU.add, op1=ALU.mult), name)
                if it.outs and step == 14:
                    it.wait(dve, x1_hi_ready, 1, -1, 1)
                    it.take(TT(x1_lo[:, :], it.ps("x1")[:, :], x1_hi[:, :].bitcast(f32), ALU.subtract), "x1")
                if it.ins and step == 16:
                    it.wait(dve, conv_th_ready, 1, 1, 1)
                    STT(out=u2[it.next][:, :, :], in0=conv_th[:, :, :], scalar=1.0, in1=conv[:, :, :],
                        op0=ALU.add, op1=ALU.mult).then_inc(u2_ready, 1)
                if it.scan and step == 19:
                    combine(it, 0, 0)
                if it.outs:
                    for b, (at, then) in enumerate(((18, 19), (24, 25), (26, 27))):
                        if step == at:
                            it.wait(dve, g_th_ready, HID, -1, b + 1)
                            it.take(STT(out=g_act[:, b, :], in0=g_th[:, b % 2, :], scalar=1.0,
                                        in1=it.ps(f"gate{b}")[:, :], op0=ALU.add, op1=ALU.mult), f"gate{b}")
                        if step == then:
                            it.wait_full(dve, f"up{b}")
                            it.wait_taken(dve, f"gate{b}")
                            it.take(TT(g_act[:, b, :], g_act[:, b, :], it.ps(f"up{b}")[:, :], ALU.mult), f"up{b}")
                if it.ins and step == 23:
                    it.wait(dve, z_step, 3, 1, 3)
                    TS(z_w[:], z_e[:], 1.0, -1.0, ALU.add, ALU.add).then_inc(soft_step, 1)
                    it.wait(dve, soft_step, 3, 1, 1)
                    TT(z_c[:], z_e[:], z_w[:], ALU.subtract).then_inc(soft_step, 1)
                if it.ins and step == 25:
                    it.wait(dve, z_ln_ready, 1, 1, 1)
                    it.wait_taken(dve, "z1")
                    it.wait(dve, soft_step, 3, 1, 2)
                    TT(z_w[:], z_ln[:], z_c[:], ALU.add).then_inc(soft_step, 1)
                    it.wait(dve, soft_step, 3, 1, 3)
                    TT(delta[:], z_w[:], z_pos[:], ALU.add).then_inc(delta_ready, 1)
                    it.wait(dve, delta_ready, 1, 1, 1)
                    TT(du[:], delta[:], u2[it.next][:], ALU.mult).then_inc(du_ready, 1)
                if it.outs:
                    if step in (29, 30):
                        for n in [step - 29]:
                            it.wait_full(dve, f"down{n}")
                            it.take(STT(out=r2[:, 2 * n:2 * n + 2, :],
                                        in0=it.ps(f"down{n}")[:, 0:2 * M].rearrange("p (i m) -> p i m", m=M),
                                        scalar=SILU2, in1=x1[:, 2 * n:2 * n + 2, :],
                                        op0=ALU.mult, op1=ALU.add), f"down{n}")
                    if step == 30:
                        for n in range(2):
                            it.wait_taken(dve, f"down{n}")
                        for i in range(TILES):
                            last = dve.bn_stats(st2[:, i, :], r2[:, i, :])
                        last.then_inc(ln2_step, 1)
                    if step == 31:
                        for i in range(TILES):
                            last = dve.bn_aggr(mv2[:, i, :], st2[:, i, :])
                        last.then_inc(ln2_step, 1)
                        it.wait(dve, ln2_step, 2, -1, 2)
                        TS(ve2[:, :], mv2[:, :, 1], EPS, None, ALU.add).then_inc(ve2_ready, 1)

            def finish(it):
                dve.wait_ge(y_free[it.next], 16 + 16 * ((it.k0 - 1) // 2) + 8 * it.ahead)
                normalise(it, y_out[it.next], r2, mv2, rs2, rs2_ready, y_ready)

            def iteration(it):
                for n in range(GROUPS):
                    if it.outs and n in (7, 31):
                        it.wait(dve, ln1_step if n == 7 else ln2_step, 2, -1, 1)
                    if it.scan:
                        scan(it, n)
                        if n % 4 == 3:
                            weigh(it, n // 4)
                    dense(it, n)
                if it.outs:
                    finish(it)
                if it.k0 == -1:
                    late_setup()

            run(dve, iteration)


_NAMES = ["x", "norm_w", "in_proj_w", "conv_w", "conv_b", "x_proj_w", "dt_proj_w", "dt_proj_b", "A_log", "D",
          "out_proj_w"]
_INS = ["L0_attn_" + n for n in _NAMES] + ["L0_ffn_w_gate", "L0_ffn_w_up", "L0_ffn_w_down"]


def kernel(**inputs):
    import numpy as np
    import concourse.bacc as bacc
    from concourse.bass_utils import run_bass_kernel_spmd

    nc = bacc.Bacc("TRN2", target_bir_lowering=False, num_devices=1)
    arrays, args = {}, []
    for name in _INS:
        a = np.ascontiguousarray(inputs[name])
        arrays[name + "_in"] = a
        args.append(nc.dram_tensor(name + "_in", a.shape, mybir.dt.from_np(a.dtype), kind="ExternalInput").ap())
    shape = np.shape(inputs["L0_attn_x"])
    out = nc.dram_tensor("out_dram", shape, mybir.dt.float32, kind="ExternalOutput").ap()
    mamba_swiglu_postln(nc, *args, out)
    r = run_bass_kernel_spmd(nc, [arrays], core_ids=[0])
    return r.results[0]["out_dram"]
```
